# Optimizing a Trainium2 kernel written in Bass

```python
import numpy as np
import jax
import jax.numpy as jnp

def _softmax(x, axis=-1):
    return jax.nn.softmax(x, axis=axis)

def _gelu(x):
    return jax.nn.gelu(x, approximate=True)

def _silu(x):
    return jax.nn.silu(x)

def _sigmoid(x):
    return jax.nn.sigmoid(x)

def _layernorm(x, axis=-1, eps=1e-05):
    m = jnp.mean(x, axis=axis, keepdims=True)
    v = jnp.var(x, axis=axis, keepdims=True)
    return (x - m) / jnp.sqrt(v + eps)

def _scatter_add(tgt, idx, src, axis=0):
    return tgt.at[idx].add(src)

def _segment_sum(src, seg, n):
    return jax.ops.segment_sum(src, seg, n)
kernel_name = 'mk_xattn_ffn_d1_seqx_r4_5bc9c3'

def setup_inputs(seed: int=0):
    np.random.seed(seed)
    _w = jnp.asarray

    def _rec_inputs():
        import jax
        import jax.numpy as jnp
        _rk = jax.random.key(seed)
        x = -7.109e-05 + 0.9999 * jax.random.normal(jax.random.fold_in(_rk, 1), (4, 512, 512), jnp.float32)
        _lenS = 512 - jax.random.randint(jax.random.fold_in(_rk, 7), (4,), 0, max(1, 512 // 4) + 1, jnp.int32)
        _lenS2 = 512 - jax.random.randint(jax.random.fold_in(_rk, 8), (4,), 0, max(1, 512 // 4) + 1, jnp.int32)
        _ctx_2048P = jax.random.normal(jax.random.fold_in(_rk, 11), (4, 16, 512), jnp.float32)
        _ctx_2048c = jax.random.dirichlet(jax.random.fold_in(_rk, 511), 0.3 * jnp.ones((16,), jnp.float32), (4, 512))
        _ctx_2048t = jnp.einsum('bsk,bkd->bsd', _ctx_2048c, _ctx_2048P)
        _ctx_2048t = _ctx_2048t * jax.lax.rsqrt(jnp.mean(jnp.square(_ctx_2048t)) + 1e-12) * 0.953939
        ctx_2048 = -3.05549e-07 + 0.0199987 * (_ctx_2048t + 0.3 * jax.random.normal(jax.random.fold_in(_rk, 611), (4, 512, 512), jnp.float32))
        return (x, ctx_2048)
    x, ctx_2048 = _rec_inputs()

    def _L0_xattn_setup():
        import jax, jax.numpy as jnp
        import numpy as np
        FP8_MAX = 448.0
        ACT_EPS = 0.0001
        W_EPS = 1e-06
        BLK = 128

        def quant_dequant_act_1x128(x):
            E, M, K = x.shape
            xb = x.reshape(E, M, K // BLK, BLK)
            amax = jnp.max(jnp.abs(xb), axis=-1, keepdims=True)
            safe = jnp.maximum(amax, ACT_EPS)
            q = (xb * (FP8_MAX / safe)).astype(jnp.float8_e4m3fn)
            return (q.astype(jnp.float32) * (safe / FP8_MAX)).reshape(E, M, K)

        def quant_dequant_weight_128x128(w):
            E, N, K = w.shape
            wb = w.reshape(E, N // BLK, BLK, K // BLK, BLK)
            amax = jnp.max(jnp.abs(wb), axis=(2, 4), keepdims=True)
            safe = jnp.maximum(amax, W_EPS)
            q = (wb * (FP8_MAX / safe)).astype(jnp.float8_e4m3fn)
            return (q.astype(jnp.float32) * (safe / FP8_MAX)).reshape(E, N, K)
        key = jax.random.key(seed)
        kx, kw = jax.random.split(key)
        E, M, K, N = (8, 1024, 512, 512)
        x = jax.random.normal(kx, (E, M, K), dtype=jnp.float32)
        weight = jax.random.normal(kw, (E, N, K), dtype=jnp.float32) * 0.02
        return {'x': x, 'weight': weight}
    _L0_xattn_all = _L0_xattn_setup()
    _L0_xattn_in = {k: v for k, v in _L0_xattn_all.items() if k in ()}
    del _L0_xattn_all

    def _L0_ffn_setup():
        import jax, jax.numpy as jnp
        import numpy as np
        B, S, D, H = (4, 512, 512, 2048)

        def fwht(x):
            orig_shape = x.shape
            n = orig_shape[-1]
            x = x.reshape(-1, n)
            h = 1
            while h < n:
                xb = x.reshape(-1, n // (2 * h), 2, h)
                a = xb[:, :, 0, :]
                b = xb[:, :, 1, :]
                x = jnp.stack([a + b, a - b], axis=2).reshape(-1, n)
                h *= 2
            scale = jnp.asarray(1.0 / np.sqrt(n), dtype=x.dtype)
            return (x * scale).reshape(orig_shape)
        key = jax.random.key(seed)
        kx, k1, k2, k3 = jax.random.split(key, 4)
        x = jax.random.normal(kx, (B, S, D), dtype=jnp.float32)
        W1 = jax.random.normal(k1, (H, D), dtype=jnp.float32) * (1.0 / np.sqrt(D))
        W2 = jax.random.normal(k2, (D, H), dtype=jnp.float32) * (1.0 / np.sqrt(H))
        W3 = jax.random.normal(k3, (H, D), dtype=jnp.float32) * (1.0 / np.sqrt(D))
        return {'x': x, 'W1': W1, 'W2': W2, 'W3': W3}
    _L0_ffn_all = _L0_ffn_setup()
    _L0_ffn_in = {k: v for k, v in _L0_ffn_all.items() if k in ('W1', 'W2', 'W3')}
    del _L0_ffn_all
    return {'x': x, 'ctx_2048': ctx_2048, 'L0_ffn_W1': _L0_ffn_in['W1'], 'L0_ffn_W2': _L0_ffn_in['W2'], 'L0_ffn_W3': _L0_ffn_in['W3']}

def reference(x, ctx_2048, L0_ffn_W1, L0_ffn_W2, L0_ffn_W3):
    import jax
    import jax.numpy as jnp

    def _L0_xattn_ref(x, weight):
        import jax, jax.numpy as jnp
        import numpy as np
        FP8_MAX = 448.0
        ACT_EPS = 0.0001
        W_EPS = 1e-06
        BLK = 128

        def quant_dequant_act_1x128(x):
            E, M, K = x.shape
            xb = x.reshape(E, M, K // BLK, BLK)
            amax = jnp.max(jnp.abs(xb), axis=-1, keepdims=True)
            safe = jnp.maximum(amax, ACT_EPS)
            q = (xb * (FP8_MAX / safe)).astype(jnp.float8_e4m3fn)
            return (q.astype(jnp.float32) * (safe / FP8_MAX)).reshape(E, M, K)

        def quant_dequant_weight_128x128(w):
            E, N, K = w.shape
            wb = w.reshape(E, N // BLK, BLK, K // BLK, BLK)
            amax = jnp.max(jnp.abs(wb), axis=(2, 4), keepdims=True)
            safe = jnp.maximum(amax, W_EPS)
            q = (wb * (FP8_MAX / safe)).astype(jnp.float8_e4m3fn)
            return (q.astype(jnp.float32) * (safe / FP8_MAX)).reshape(E, N, K)
        xq = quant_dequant_act_1x128(x)
        wq = quant_dequant_weight_128x128(weight)
        return jnp.einsum('emk,enk->emn', xq, wq)

    def _L0_ffn_ref(x, W1, W2, W3):
        import jax, jax.numpy as jnp
        import numpy as np
        B, S, D, H = (4, 512, 512, 2048)

        def fwht(x):
            orig_shape = x.shape
            n = orig_shape[-1]
            x = x.reshape(-1, n)
            h = 1
            while h < n:
                xb = x.reshape(-1, n // (2 * h), 2, h)
                a = xb[:, :, 0, :]
                b = xb[:, :, 1, :]
                x = jnp.stack([a + b, a - b], axis=2).reshape(-1, n)
                h *= 2
            scale = jnp.asarray(1.0 / np.sqrt(n), dtype=x.dtype)
            return (x * scale).reshape(orig_shape)
        up_gate = jnp.einsum('bsd,hd->bsh', x, W1)
        up_lin = jnp.einsum('bsd,hd->bsh', x, W3)
        hidden = jax.nn.silu(up_gate) * up_lin
        hidden = fwht(hidden)
        out = jnp.einsum('bsh,dh->bsd', hidden, W2)
        return out
    x = x + _L0_xattn_ref(_layernorm(x, axis=-1), ctx_2048)
    x = x + _L0_ffn_ref(_layernorm(x, axis=-1), L0_ffn_W1, L0_ffn_W2, L0_ffn_W3)
    return x

_drawn_inputs = setup_inputs


def setup_inputs(seed=0):
    import zlib

    import numpy as np

    out = dict(_drawn_inputs(seed))
    spreads = {}
    factors = {}
    for name, (base, spread) in spreads.items():
        noise = np.random.default_rng([zlib.crc32(name.encode()), seed]).standard_normal(out[name].shape)
        drawn = base * np.exp(spread * noise) if base else spread * noise
        out[name] = jnp.asarray(drawn.astype(out[name].dtype))
    for name, factor in factors.items():
        out[name] = (out[name] * factor).astype(out[name].dtype)
    return out
```

```python
from contextlib import ExitStack, contextmanager

import concourse.bass as bass
from concourse import mybir

F32 = mybir.dt.float32
F16 = mybir.dt.float16
I32 = mybir.dt.int32
ALU = mybir.AluOpType
ACT = mybir.ActivationFunctionType
AX_X = mybir.AxisListType.X
RMAX = bass.bass_isa.ReduceOp.max

P = 128
FP8_MAX = 448.0
ACT_EPS, W_EPS, LN_EPS = 1e-4, 1e-6, 1e-5
EXPONENT = 0x7F800000
ONE = 1 << 23
ROUNDER = 1.5 * 2.0 ** 20
LEAST_NORMAL = 2.0 ** -6
Z_SCALE = 2.0 ** 11


class Count:

    def __init__(self):
        self.base, self.n = 0, 0

    def next(self):
        self.n += 1
        return self.base + self.n

    @contextmanager
    def loop(self, index, trips, each):
        base, n = self.base, self.n
        self.base, self.n = base + index * each + n, 0
        yield
        assert self.n == each, f"{self.n} steps a trip, not {each}"
        self.base, self.n = base, n + trips * each


def cols(t, start, n):
    return t[:, bass.ds(start, n)]


def blocks(ap):
    return ap.rearrange("p (k n) -> p k n", n=P)


def xattn_ffn(nc, x, ctx_w, w1, w2, w3, eye32_in, eye16_in, had_in, out):
    NB, S, D = x.shape
    H = w1.shape[0]
    KC = D // P
    TI = S // P
    HC = H // P
    assert D == 512 and S == 512 and KC == 4 and TI == 4 and HC == 16 and NB >= 3
    SLOTS = 4
    AHEAD = 4
    Q_FROM = 4
    NQ = 2 * TI

    x_rows = x.rearrange("b s d -> (b s) d")
    ctx_rows = ctx_w.rearrange("b s d -> (b s) d")
    out_rows = out.rearrange("b s d -> (b s) d")

    with ExitStack() as stack:
        def sb(name, shape, dt):
            return stack.enter_context(nc.sbuf_tensor(name, shape, dt))

        def sem(name):
            return stack.enter_context(nc.semaphore(name))

        w13_hi = sb("w13_hi", [P, 2, KC, H], F16)
        w13_lo = sb("w13_lo", [P, 2, KC, H], F16)
        w2r = sb("w2r", [P, HC, 2, D], F16)
        w2_f32 = w2r[:].rearrange("p c s n -> p (c s n)").bitcast(F32)
        w2_f32c = w2_f32.rearrange("p (c n) -> p c n", c=HC)
        h_hi = sb("h_hi", [P, HC * S], F16)
        h_lo = sb("h_lo", [P, HC * S], F16)
        zt_hi = sb("zt_hi", [P, KC, S], F16)
        zt_lo = sb("zt_lo", [P, KC, S], F16)
        qt_ctx = sb("qt_ctx", [P, KC, S], F16)
        qt_x = sb("qt_x", [P, KC, S], F16)
        x_sb = sb("x_sb", [P, 2 * TI * D], F32)
        ctx_sb = sb("ctx_sb", [P, TI * D], F32)
        zb = sb("zb", [P, 2, D], F32)
        mb = sb("mb", [P, 2, D], F32)
        qb = sb("qb", [P, 2, D], F16)
        z_hl = sb("z_hl", [P, 2, D], F16)
        hid = sb("hid", [P, 2, S], F32)
        ring = sb("ring", [P, SLOTS, D], F32)
        stage = sb("stage", [P, 2, D], F32)
        fly = sb("fly", [P, HC, P], F32)
        junk = sb("junk", [P, D], F16)
        eye32 = sb("eye32", [P, P], F32)
        eye16 = sb("eye16", [P, P], F16)
        had = sb("had", [P, P], F32)
        bn = sb("bn", [P, 6], F32)
        mv1 = sb("mv1", [P, TI, 2], F32)
        mv2 = sb("mv2", [P, TI, 2], F32)
        rs1 = sb("rs1", [P, TI], F32)
        rs2 = sb("rs2", [P, TI], F32)
        nt = sb("nt", [P, 2, TI], F32)
        camax = sb("camax", [P, TI, KC], F32)
        cmax = sb("cmax", [P, TI, KC], F32)
        xamax = sb("xamax", [P, KC], F32)
        safe = sb("safe", [P, KC], F32)
        rq = sb("rq", [P, KC], F32)
        sx = sb("sx", [P, TI * KC], F32)
        sw = sb("sw", [P, TI * KC], F32)
        coef = sb("coef", [P, TI * KC * TI], F32)
        sq13 = sb("sq13", [P, HC * 2], F32)
        tb13 = sb("tb13", [P, HC * 2], F32)
        sc13 = sb("sc13", [P, HC * 2], F32)
        silu_sc = sb("silu_sc", [P, HC], F32)
        hid_sc = sb("hid_sc", [P, HC], F32)
        sq2 = sb("sq2", [P, HC], F32)
        rowmul = sb("rowmul", [P, HC], F32)
        peaks = sb("peaks", [P, 2], F32)
        gpeaks = sb("gpeaks", [P, 2], F32)
        gs = sb("gs", [P, 4], F32)
        outmul = sb("outmul", [P, 1], F32)
        credit = sb("credit", [P, 4], F32)

        ps_g = stack.enter_context(nc.psum_tensor("ps_g", [P, 2, 512], F32))
        ps_u = stack.enter_context(nc.psum_tensor("ps_u", [P, 2, 512], F32))
        ps_d = stack.enter_context(nc.psum_tensor("ps_d", [P, 2, 512], F32))
        ps_x = stack.enter_context(nc.psum_tensor("ps_x", [P, 2, 512], F32))

        passed = sem("passed")
        const_in = sem("const_in")
        ctx_in = [sem(f"ctx_in{i}") for i in range(TI)]
        x_in = [sem(f"x_in{i}") for i in range(TI)]
        w_in = [sem(f"w_in{i}") for i in range(SLOTS)]
        y_out = [sem(f"y_out{i}") for i in range(TI)]
        dve_step = sem("dve_step")
        camax_done = sem("camax_done")
        ctx_read = sem("ctx_read")
        v_done = sem("v_done")
        g_used = sem("g_used")
        zn_done = sem("zn_done")
        zlo_done = sem("zlo_done")
        out_ready = sem("out_ready")
        w_scaled = sem("w_scaled")
        w13_lo_done = sem("w13_lo_done")
        hid_done = sem("hid_done")
        hlo_done = sem("hlo_done")
        peaks_done = sem("peaks_done")
        w2_scaled = sem("w2_scaled")
        w2_lo_done = sem("w2_lo_done")
        sq_done = sem("sq_done")
        w2_staged = sem("w2_staged")
        w2_stored = sem("w2_stored")
        w13_hi_done = sem("w13_hi_done")
        silu_done = sem("silu_done")
        hhi_done = sem("hhi_done")
        q_stored = sem("q_stored")
        zhi_done = sem("zhi_done")
        zt_stored = sem("zt_stored")
        w2_hi_done = sem("w2_hi_done")
        w2_turned = sem("w2_turned")
        w2_mixed = sem("w2_mixed")
        w13_turned = sem("w13_turned")
        gate_ready = sem("gate_ready")
        up_ready = sem("up_ready")
        q_turned = sem("q_turned")
        g_ready = sem("g_ready")
        z_turned = sem("z_turned")
        down_ready = sem("down_ready")
        pool_step = sem("pool_step")
        cmax_done = sem("cmax_done")
        q_done = sem("q_done")
        fly_done = sem("fly_done")
        gpeaks_done = sem("gpeaks_done")

        def alone(eng):
            eng.sem_inc(passed, 1)

        def par(b):
            return b % 2

        def x_tile(b, i):
            return cols(x_sb, (par(b) * TI + i) * D, D)

        def gate_steps(eng, j0, j1, body, counter=None, each=0, parity0=0):
            n = j1 - j0
            if n % 2 or n < 4:
                for j in range(j0, j1):
                    body(j, j % 2, j - j0)
                return
            with eng.Fori(0, n // 2) as r:
                if counter is not None:
                    with counter.loop(r, n // 2, each):
                        for k in range(2):
                            body(j0 + k + r * 2, (j0 + k) % 2, k + r * 2)
                else:
                    for k in range(2):
                        body(j0 + k + r * 2, (j0 + k) % 2, k + r * 2)

        block = stack.enter_context(nc.Block())

        @block.sync
        def _(sp):
            def load_batch(b):
                for i in range(TI):
                    if not (isinstance(b, int) and b == 0):
                        sp.wait_ge(ctx_read, b * TI + i + 1 - TI)
                        alone(sp)
                        sp.wait_ge(ctx_in[i], b * 16)
                        alone(sp)
                    sp.dma_start(cols(ctx_sb, i * D, D),
                                 ctx_rows[bass.ds(b * S + i * P, P), :]).then_inc(ctx_in[i], 16)
                for i in range(TI):
                    if not (isinstance(b, int) and b == 0):
                        sp.wait_ge(x_in[i], b * 16)
                        alone(sp)
                        if not (isinstance(b, int) and b == 1):
                            sp.wait_ge(y_out[i], b * 16 - 16)
                        alone(sp)
                    sp.dma_start(x_tile(b, i), x_rows[bass.ds(b * S + i * P, P), :]).then_inc(x_in[i], 16)

            def store_batch(b):
                for i in range(TI):
                    sp.wait_ge(out_ready, b * TI + (i + 1) + 2)
                    sp.dma_start(out_rows[bass.ds(b * S + i * P, P), :], x_tile(b, i)).then_inc(y_out[i], 16)

            def load_w2(dc, hq, wait):
                if wait:
                    sp.wait_ge(w2_turned, dc * 4 + hq - SLOTS + 1)
                    sp.wait_ge(sq_done, dc * 4 + hq - SLOTS + 1)
                sp.dma_start(ring[:, hq, :], w2[bass.ds(dc * P, P), hq * 512:(hq + 1) * 512]).then_inc(w_in[hq], 16)

            def load_w13(j, k, wait):
                for w, src in enumerate((w1, w3)):
                    slot = 2 * k + w
                    if wait:
                        sp.wait_ge(w13_turned, j * 2 + w - SLOTS + 1)
                    sp.dma_start(ring[:, slot, :], src[bass.ds(j * P, P), :]).then_inc(w_in[slot], 16)

            load_batch(0)
            sp.dma_start(eye32[:], eye32_in).then_inc(const_in, 16)
            sp.dma_start(eye16[:], eye16_in).then_inc(const_in, 16)
            sp.dma_start(had[:], had_in).then_inc(const_in, 16)
            for hq in range(4):
                load_w2(0, hq, False)
            with sp.Fori(1, KC) as dc:
                for hq in range(4):
                    load_w2(dc, hq, True)
            for j in range(2):
                for w in range(2):
                    sp.wait_ge(w2_turned, 4 * KC - SLOTS + 2 * j + w + 1)
                    sp.wait_ge(sq_done, 4 * KC - SLOTS + 2 * j + w + 1)
                load_w13(j, j, False)
            load_w13(2, 0, True)
            load_w13(3, 1, True)
            load_batch(1)
            with sp.Fori(AHEAD // 2, HC // 2) as r:
                for k in range(2):
                    load_w13(r * 2 + k, k, True)
            store_batch(0)
            with sp.Fori(1, NB - 1) as b:
                load_batch(b + 1)
                store_batch(b)
            store_batch(NB - 1)
            for i in range(TI):
                sp.wait_ge(y_out[i], 16 * NB)

        @block.tensor
        def _(pe):
            def turn_w2(t, hq):
                pe.wait_ge(w_in[hq], t // 4 * 16 + 16)
                if t > 0:
                    pe.wait_ge(w2_staged, t)
                for k in range(4):
                    last = nc.tensor.transpose(ps_d[:, 0, k * P:(k + 1) * P],
                                               ring[:, hq, k * P:(k + 1) * P], eye32[:])
                last.then_inc(w2_turned, 1)

            def mix_w2(t):
                pe.wait_ge(w2_staged, t + 1)
                if t > 0:
                    pe.wait_ge(w2_stored, t)
                nc.tensor.matmul(ps_d[:, 1, :], had[:], stage[:, t % 2, :],
                                 start=True, stop=True).then_inc(w2_mixed, 1)

            def turn_w13(j, k, first=False):
                for w in range(2):
                    pe.wait_ge(w_scaled, j * 2 + w + 1)
                    if first:
                        pe.wait_ge(w2_stored, HC)
                    else:
                        pe.wait_ge(w13_lo_done, j * 2 + w - 1)
                    for c in range(KC):
                        last = nc.tensor.transpose(ps_d[:, w, c * P:(c + 1) * P],
                                                   ring[:, 2 * k + w, c * P:(c + 1) * P], eye32[:])
                    last.then_inc(w13_turned, 1)

            def turn_q(b, u, k, free):
                pe.wait_ge(q_done, b * NQ + u + 1)
                if free is not None:
                    pe.wait_ge(*free)
                for c in range(KC):
                    last = nc.tensor.transpose(ps_x[:, k, 0:D // 2].bitcast(F16)[:, c * P:(c + 1) * P],
                                               qb[:, k, c * P:(c + 1) * P], eye16[:])
                last.then_inc(q_turned, 1)

            def block_product(b, i, kb, bank):
                nc.tensor.matmul(bank, qt_x[:, kb, bass.ds(i * P, P)], qt_ctx[:, kb, :],
                                 start=True, stop=True).then_inc(g_ready, 1)

            def turn_z(b, i, free):
                pe.wait_ge(zlo_done, b * TI + i + 1)
                if free is not None:
                    pe.wait_ge(*free)
                for s in range(2):
                    for c in range(KC):
                        last = nc.tensor.transpose(ps_x[:, s, 0:D // 2].bitcast(F16)[:, c * P:(c + 1) * P],
                                                   z_hl[:, s, c * P:(c + 1) * P], eye16[:])
                last.then_inc(z_turned, 1)

            def project(bank, w, j, done):
                n = 0
                for c in range(KC):
                    for wt, zt in ((w13_hi, zt_hi), (w13_hi, zt_lo), (w13_lo, zt_hi)):
                        last = nc.tensor.matmul(bank, wt[:, w, c, bass.ds(j * P, P)], zt[:, c, :],
                                                start=n == 0, stop=n == 3 * KC - 1)
                        n += 1
                last.then_inc(done, 1)

            def gate_phase(b, weights, following):
                pe.wait_ge(zt_stored, b * TI + TI)
                alone(pe)

                def chunk(j, k, prep, turn_u):
                    pe.wait_ge(silu_done, b * HC + j + 1)
                    project(ps_g[:, k, :], 0, j, gate_ready)
                    if prep:
                        turn_w13(j + AHEAD, k)
                    pe.wait_ge(hid_done, b * HC + j + 1)
                    project(ps_u[:, k, :], 1, j, up_ready)
                    if turn_u is not None:
                        turn_q(b + 1, turn_u, k, (q_stored, (b + 1) * NQ + turn_u - 1))

                gate_steps(pe, 0, Q_FROM, lambda j, k, n: chunk(j, k, weights, None))
                if following:
                    gate_steps(pe, Q_FROM, Q_FROM + NQ, lambda j, k, n: chunk(j, k, weights, n))
                else:
                    gate_steps(pe, Q_FROM, Q_FROM + NQ, lambda j, k, n: chunk(j, k, weights, None))
                gate_steps(pe, Q_FROM + NQ, HC, lambda j, k, n: chunk(j, k, False, None))

            def down_phase(b, first, following):
                def tile(i, k):
                    if first:
                        pe.wait_ge(w13_lo_done, 2 * HC)
                    pe.wait_ge(out_ready, b * TI + i + 1)
                    n = 0
                    for c in range(HC):
                        pe.wait_ge(hlo_done, b * HC + (c + 1) + 2)
                        if first:
                            pe.wait_ge(w2_lo_done, c + 1)
                        for ht, s in ((h_hi, 0), (h_hi, 1), (h_lo, 0)):
                            last = nc.tensor.matmul(ps_d[:, k, :], ht[:, bass.ds(i * P + c * S, P)], w2r[:, c, s, :],
                                                    start=n == 0, stop=n == 3 * HC - 1)
                            n += 1
                        if following and c in (1, 2, 5, 8):
                            kb = (1, 2, 5, 8).index(c)
                            g = (b + 1) * TI * KC + i * KC + kb
                            if kb < 2:
                                pe.wait_ge(q_stored, (b + 1) * NQ + NQ)
                                pe.wait_ge(zt_stored, (b + 1) * TI + i)
                            else:
                                pe.wait_ge(g_used, g - 1)
                            block_product(b + 1, i, kb, ps_x[:, kb % 2, :])
                        if following and c == HC - 2:
                            turn_z(b + 1, i, None)
                    last.then_inc(down_ready, 1)

                with pe.Fori(0, TI // 2) as r:
                    for k in range(2):
                        tile(r * 2 + k, k)

            pe.wait_ge(const_in, 48)
            for t in range(HC):
                turn_w2(t, t % 4)
                if t:
                    mix_w2(t - 1)
                if t >= 8:
                    turn_q(0, t - 8, t % 2, (q_stored, t - 9) if t >= 10 else None)
            mix_w2(HC - 1)
            for j in range(AHEAD):
                turn_w13(j, j % 2, first=j == 0)
            pe.wait_ge(q_stored, NQ)
            for i in range(TI):
                for kb in range(KC):
                    g = i * KC + kb
                    if g >= 4:
                        pe.wait_ge(g_used, g - 3)
                    block_product(0, i, kb, (ps_g if kb < 2 else ps_u)[:, kb % 2, :])
            for i in range(TI):
                turn_z(0, i, (zt_stored, i) if i else None)
            pe.wait_ge(g_used, TI * KC)
            gate_phase(0, True, True)
            down_phase(0, True, True)
            with pe.Fori(1, NB - 1) as b:
                gate_phase(b, False, True)
                down_phase(b, False, True)
            gate_phase(NB - 1, False, False)
            down_phase(NB - 1, False, False)

        @block.scalar
        def _(act):
            def store_q(b, u, k, dst, i):
                act.wait_ge(q_turned, b * NQ + u + 1)
                nc.scalar.copy(dst[:, :, bass.ds(i * P, P)],
                               blocks(ps_x[:, k, 0:D // 2].bitcast(F16))).then_inc(q_stored, 1)

            def split_w13(j):
                for w in range(2):
                    act.wait_ge(w13_turned, j * 2 + w + 1)
                    nc.scalar.copy(w13_hi[:, w, :, bass.ds(j * P, P)], blocks(ps_d[:, w, :])).then_inc(w13_hi_done, 1)

            def norm_w13(j, k):
                for w in range(2):
                    slot = 2 * k + w
                    act.wait_ge(w_in[slot], (KC + 1) * 16 + (j - k) // 2 * 16 if isinstance(j, int)
                                else (KC + 1) * 16 + (j - k) * 8)
                    act.wait_ge(sq_done, j * 2 + (w + HC))
                    nc.scalar.activation(junk[:], ring[:, slot, :], ACT.Square,
                                         accum_out=cols(sq13, j * 2 + w, 1)).then_inc(sq_done, 1)

            def z_high(b, i, k):
                act.wait_ge(zn_done, b * TI + i + 1)
                if not (isinstance(b, int) and b == 0 and isinstance(i, int) and i == 0):
                    act.wait_ge(z_turned, b * TI + i)
                nc.scalar.mul(z_hl[:, 0, :], zb[:, k, :], Z_SCALE).then_inc(zhi_done, 1)

            def store_z(b, i):
                act.wait_ge(z_turned, b * TI + i + 1)
                for s, dst in enumerate((zt_hi, zt_lo)):
                    last = nc.scalar.copy(dst[:, :, bass.ds(i * P, P)], blocks(ps_x[:, s, 0:D // 2].bitcast(F16)))
                last.then_inc(zt_stored, 1)

            def gate_phase(b, weights, following):
                def chunk(j, k, prep, q, convert):
                    if prep:
                        norm_w13(j + AHEAD, k)
                    if convert is not None:
                        convert_high(convert, 0)
                    act.wait_ge(gate_ready, b * HC + j + 1)
                    act.wait_ge(hlo_done, b * HC + j + 1)
                    nc.scalar.activation(hid[:, k, :], ps_g[:, k, :], ACT.Silu,
                                         scale=cols(silu_sc, j, 1)).then_inc(silu_done, 1)
                    if prep:
                        split_w13(j + AHEAD)
                    if convert is not None:
                        convert_high(convert, 2)
                    act.wait_ge(hid_done, b * HC + (j + 1) + 2)
                    nc.scalar.copy(cols(h_hi, j * S, S), hid[:, k, :]).then_inc(hhi_done, 1)
                    if q is not None:
                        u, dst, i = q
                        store_q(b + 1, u, k, dst, i)

                def convert_high(n, c0):
                    for c in range(c0, c0 + 2):
                        act.wait_ge(w2_scaled, n * 4 + (c + 1))
                        nc.scalar.copy(w2r[:].rearrange("p c s n -> p (c s n)")[:, bass.ds((n * 4 + c) * 2 * D, D)],
                                       stage[:, c % 2, :]).then_inc(w2_hi_done, 1)

                half = Q_FROM + TI
                gate_steps(act, 0, Q_FROM, lambda j, k, n: chunk(j, k, weights, None, None))
                gate_steps(act, Q_FROM, half,
                           lambda j, k, n: chunk(j, k, weights, (n, qt_ctx, n) if following else None, None),)
                gate_steps(act, half, Q_FROM + NQ,
                           lambda j, k, n: chunk(j, k, weights, (n + TI, qt_x, n) if following else None, None),)
                gate_steps(act, Q_FROM + NQ, HC, lambda j, k, n: chunk(j, k, False, None, n if weights else None))

            def down_phase(b):
                with act.Fori(0, TI // 2) as r:
                    for k in range(2):
                        z_high(b + 1, r * 2 + k, k)
                        store_z(b + 1, r * 2 + k)

            for t in range(HC):
                dc, hq = t // 4, t % 4
                act.wait_ge(w_in[hq], dc * 16 + 16)
                if t:
                    act.wait_ge(sq_done, t)
                nc.scalar.activation(junk[:], ring[:, hq, :], ACT.Square,
                                     accum_out=sq2[:, t:t + 1]).then_inc(sq_done, 1)
                act.wait_ge(w2_turned, t + 1)
                if t >= 2:
                    act.wait_ge(w2_mixed, t - 1)
                nc.scalar.copy(stage[:, t % 2, :], ps_d[:, 0, :]).then_inc(w2_staged, 1)
                if t:
                    s = t - 1
                    act.wait_ge(w2_mixed, s + 1)
                    nc.scalar.copy(w2_f32c[:, 4 * (s % 4):4 * (s % 4) + 4, (s // 4) * P:(s // 4 + 1) * P],
                                   blocks(ps_d[:, 1, :])).then_inc(w2_stored, 1)
                if t >= 8:
                    u = t - 8
                    store_q(0, u, u % 2, qt_ctx if u < TI else qt_x, u % TI)
            act.wait_ge(w2_mixed, HC)
            nc.scalar.copy(w2_f32c[:, HC - 4:HC, (KC - 1) * P:KC * P], blocks(ps_d[:, 1, :])).then_inc(w2_stored, 1)
            for j in range(AHEAD):
                norm_w13(j, j % 2)
                split_w13(j)
            for i in range(TI):
                z_high(0, i, i % 2)
                store_z(0, i)
            gate_phase(0, True, True)
            down_phase(0)
            with act.Fori(1, NB - 1) as b:
                gate_phase(b, False, True)
                down_phase(b)
            gate_phase(NB - 1, False, False)

        @block.gpsimd
        def _(pool):
            step = Count()

            def block_max(b, i, s):
                pool.wait_ge(camax_done, b * TI + i + 1)
                alone(pool)
                nc.gpsimd.partition_all_reduce(cmax[:, s, :], camax[:, s, :], P, RMAX).then_inc(cmax_done, 1)

            def round_tile(b, u, k):
                pool.wait_ge(v_done, b * NQ + u + 1)
                nc.gpsimd.tensor_tensor(zb[:, k, :], zb[:, k, :], mb[:, k, :], ALU.add).then_inc(pool_step, 1)
                if not (isinstance(b, int) and b == 0 and u < 2):
                    pool.wait_ge(q_turned, b * NQ + u - 1)
                pool.wait_ge(pool_step, step.next())
                nc.gpsimd.tensor_tensor(qb[:, k, :], zb[:, k, :], mb[:, k, :], ALU.subtract).then_inc(q_done, 1)

            def butterfly(dc, n):
                stride, op = 1 << (n // 2), (ALU.add, ALU.subtract)[n % 2]
                a = w2_f32c[:, :, dc * P:(dc + 1) * P]
                src, dst = (a, fly[:]) if n // 2 % 2 == 0 else (fly[:], a)
                sv = src.rearrange("p (a t r) d -> p a t r d", t=2, r=stride)
                dv = dst.rearrange("p (a t r) d -> p a t r d", t=2, r=stride)
                if n == 0:
                    pool.wait_ge(w2_stored, 4 * dc + 4)
                    if dc:
                        pool.wait_ge(fly_done, dc)
                elif n % 2 == 0:
                    pool.wait_ge(pool_step, step.base + step.n)
                if stride == 1:
                    o, x0, x1 = dv[:, :, n % 2, 0, :], sv[:, :, 0, 0, :], sv[:, :, 1, 0, :]
                elif stride == 8:
                    o, x0, x1 = dv[:, 0, n % 2, :, :], sv[:, 0, 0, :, :], sv[:, 0, 1, :, :]
                else:
                    o, x0, x1 = dv[:, :, n % 2, :, :], sv[:, :, 0, :, :], sv[:, :, 1, :, :]
                last = nc.gpsimd.tensor_tensor(o, x0, x1, op)
                if n < 7:
                    last.then_inc(pool_step, 1)
                    step.next()
                else:
                    last.then_inc(fly_done, 1)

            for i in range(TI):
                block_max(0, i, i)
                if i:
                    round_tile(0, i - 1, (i - 1) % 2)
            for u in range(TI - 1, NQ):
                round_tile(0, u, u % 2)
            for dc in range(2):
                for n in range(8):
                    butterfly(dc, n)
            for u in range(NQ):
                if u < TI:
                    block_max(1, u, u % 2)
                round_tile(1, u, u % 2)
                butterfly(2 + u // 4, 2 * (u % 4))
                butterfly(2 + u // 4, 2 * (u % 4) + 1)
            pool.wait_ge(peaks_done, 1)
            nc.gpsimd.partition_all_reduce(gpeaks[:], peaks[:], P, RMAX).then_inc(gpeaks_done, 1)
            with pool.Fori(2, NB) as b:
                with step.loop(b - 2, NB - 2, NQ):
                    for u0 in (0, TI):
                        with pool.Fori(0, TI // 2) as r:
                            with step.loop(r, TI // 2, 2):
                                for k in range(2):
                                    if u0 == 0:
                                        block_max(b, r * 2 + k, k)
                                    round_tile(b, r * 2 + (u0 + k), k)

        @block.vector
        def _(dve):
            step = Count()

            def inverse_root(var, root, n):
                ve, t = nt[:, 0, 0:n], nt[:, 1, 0:n]
                nc.vector.tensor_scalar(ve, var, LN_EPS, None, ALU.add).then_inc(dve_step, 1)
                dve.wait_ge(dve_step, step.next())
                nc.vector.tensor_scalar(t.bitcast(I32), ve.bitcast(I32), 1, None,
                                        ALU.logical_shift_right).then_inc(dve_step, 1)
                dve.wait_ge(dve_step, step.next())
                nc.vector.tensor_scalar(root.bitcast(I32), t.bitcast(I32), -1.0, float(0x5F3759DF), ALU.mult,
                                        ALU.add).then_inc(dve_step, 1)
                dve.wait_ge(dve_step, step.next())
                for _ in range(3):
                    nc.vector.scalar_tensor_tensor(out=t, in0=root, scalar=-0.5, in1=root, op0=ALU.mult,
                                                   op1=ALU.mult).then_inc(dve_step, 1)
                    dve.wait_ge(dve_step, step.next())
                    nc.vector.tensor_tensor(t, t, ve, ALU.mult).then_inc(dve_step, 1)
                    dve.wait_ge(dve_step, step.next())
                    nc.vector.scalar_tensor_tensor(out=root, in0=t, scalar=1.5, in1=root, op0=ALU.add,
                                                   op1=ALU.mult).then_inc(dve_step, 1)
                    dve.wait_ge(dve_step, step.next())
                alone(dve)

            def row_stats(src, mv):
                alone(dve)
                nc.vector.bn_stats(bn[:], src).then_inc(dve_step, 1)
                dve.wait_ge(dve_step, step.next())
                alone(dve)
                nc.vector.bn_aggr(mv, bn[:]).then_inc(dve_step, 1)
                dve.wait_ge(dve_step, step.next())
                alone(dve)

            def x_stats(b, tiles):
                for i in tiles:
                    dve.wait_ge(x_in[i], b * 16 + 16)
                    row_stats(x_tile(b, i), mv1[:, i, :])

            def context_max(b, i, s):
                if isinstance(i, int):
                    dve.wait_ge(ctx_in[i], b * 16 + 16)
                nc.vector.tensor_reduce(camax[:, s, :], blocks(cols(ctx_sb, i * D, D)), AX_X, ALU.max,
                                        apply_absolute_value=True).then_inc(camax_done, 1)

            def quantise(b, u, i, k, s, free):
                context = s is not None
                src = cols(ctx_sb, i * D, D) if context else x_tile(b, i)
                eps, scales = (W_EPS, sw) if context else (ACT_EPS, sx)
                z = zb[:, k, :]
                if free:
                    dve.wait_ge(q_done, b * NQ + u - 1)
                if context:
                    dve.wait_ge(cmax_done, b * TI + i + 1)
                    peak = cmax[:, s, :]
                else:
                    nc.vector.tensor_scalar(z, src, mv1[:, :, 0:1].rearrange("p a b -> p (a b)")[:, bass.ds(i, 1)],
                                            cols(rs1, i, 1), ALU.subtract, ALU.mult).then_inc(dve_step, 1)
                    dve.wait_ge(dve_step, step.next())
                    src, peak = z, xamax[:]
                    nc.vector.tensor_reduce(peak, blocks(z), AX_X, ALU.max,
                                            apply_absolute_value=True).then_inc(dve_step, 1)
                    dve.wait_ge(dve_step, step.next())
                nc.vector.tensor_scalar(safe[:], peak, eps, None, ALU.max).then_inc(dve_step, 1)
                dve.wait_ge(dve_step, step.next())
                nc.vector.reciprocal(rq[:], safe[:]).then_inc(dve_step, 1)
                nc.vector.tensor_scalar(cols(scales, i * KC, KC), safe[:], 1.0 / FP8_MAX, None,
                                        ALU.mult).then_inc(dve_step, 1)
                step.next()
                dve.wait_ge(dve_step, step.next())
                nc.vector.tensor_scalar(rq[:], rq[:], FP8_MAX, None, ALU.mult).then_inc(dve_step, 1)
                dve.wait_ge(dve_step, step.next())
                scaled = nc.vector.tensor_tensor(blocks(z), blocks(src), rq[:].unsqueeze(2).broadcast_to([P, KC, P]),
                                                 ALU.mult)
                if context:
                    scaled.then_inc(ctx_read, 1)
                    dve.wait_ge(ctx_read, b * TI + i + 1)
                else:
                    scaled.then_inc(dve_step, 1)
                    dve.wait_ge(dve_step, step.next())
                nc.vector.tensor_scalar(mb[:, k, :].bitcast(I32), z.bitcast(I32), EXPONENT, None,
                                        ALU.bitwise_and).then_inc(dve_step, 1)
                dve.wait_ge(dve_step, step.next())
                nc.vector.tensor_scalar(mb[:, k, :], mb[:, k, :], LEAST_NORMAL, ROUNDER, ALU.max,
                                        ALU.mult).then_inc(v_done, 1)

            def block_scales():
                shape = [P, TI, KC, TI]
                a = sx[:].rearrange("p (i k) -> p i k", i=TI).unsqueeze(3).broadcast_to(shape)
                w = sw[:].rearrange("p (n k) -> p k n", n=TI).unsqueeze(1).broadcast_to(shape)
                nc.vector.tensor_tensor(coef[:].rearrange("p (i k n) -> p i k n", i=TI, k=KC), a, w,
                                        ALU.mult).then_inc(dve_step, 1)
                dve.wait_ge(dve_step, step.next())
                alone(dve)

            def add_products(b, i, bank):
                steps = []
                for kb in range(KC):
                    done = (b * TI + i) * KC + kb
                    dve.wait_ge(g_ready, done + 1)
                    for nb in range(TI):
                        if kb and nb < TI - 1:
                            dve.wait_ge(dve_step, steps[1 - TI])
                        elif kb:
                            dve.wait_ge(g_used, done)
                        y = cols(x_sb, (par(b) * TI + i) * D + nb * P, P)
                        last = nc.vector.scalar_tensor_tensor(
                            out=y, in0=bank(kb)[:, nb * P:(nb + 1) * P],
                            scalar=cols(coef, (i * KC + kb) * TI + nb, 1), in1=y, op0=ALU.mult, op1=ALU.add)
                        if nb < TI - 1:
                            last.then_inc(dve_step, 1)
                            steps.append(step.next())
                    last.then_inc(g_used, 1)
                dve.wait_ge(g_used, (b * TI + i) * KC + KC)

            def normalise(b, i, k, mv, root):
                nc.vector.tensor_scalar(zb[:, k, :], x_tile(b, i), mv, root, ALU.subtract,
                                        ALU.mult).then_inc(zn_done, 1)
                dve.wait_ge(zhi_done, b * TI + i + 1)
                dve.wait_ge(zn_done, b * TI + i + 1)
                nc.vector.scalar_tensor_tensor(out=z_hl[:, 1, :], in0=zb[:, k, :], scalar=Z_SCALE, in1=z_hl[:, 0, :],
                                               op0=ALU.mult, op1=ALU.subtract).then_inc(zlo_done, 1)

            def bits(dst, src, n, m):
                nc.vector.tensor_scalar(dst.bitcast(I32), src.bitcast(I32), float(n), float(m), ALU.mult,
                                        ALU.add).then_inc(dve_step, 1)

            def scale_w13(j, k):
                dve.wait_ge(sq_done, j * 2 + (2 + HC))
                t = cols(tb13, j * 2, 2)
                nc.vector.tensor_scalar(t.bitcast(I32), cols(sq13, j * 2, 2).bitcast(I32), 24, 23,
                                        ALU.logical_shift_right, ALU.logical_shift_left).then_inc(dve_step, 1)
                dve.wait_ge(dve_step, step.next())
                bits(cols(sc13, j * 2, 2), t, -1, 204 * ONE)
                bits(cols(silu_sc, j, 1), cols(tb13, j * 2, 1), 1, 39 * ONE)
                bits(cols(hid_sc, j, 1), cols(tb13, j * 2, 1), -1, 169 * ONE)
                step.next()
                step.next()
                dve.wait_ge(dve_step, step.next())
                for w in range(2):
                    tile = ring[:, 2 * k + w, :]
                    nc.vector.tensor_scalar(tile, tile, cols(sc13, j * 2 + w, 1), None, ALU.mult).then_inc(w_scaled, 1)

            def low_w13(j):
                for w in range(2):
                    dve.wait_ge(w13_hi_done, j * 2 + w + 1)
                    at = (slice(None), w, slice(None), bass.ds(j * P, P))
                    nc.vector.tensor_tensor(w13_lo[at], blocks(ps_d[:, w, :]), w13_hi[at],
                                            ALU.subtract).then_inc(w13_lo_done, 1)

            def hidden(b, j, k):
                dve.wait_ge(silu_done, b * HC + (j + 1) + 2)
                dve.wait_ge(up_ready, b * HC + j + 1)
                nc.vector.scalar_tensor_tensor(out=hid[:, k, :], in0=hid[:, k, :], scalar=cols(hid_sc, j, 1),
                                               in1=ps_u[:, k, :], op0=ALU.mult, op1=ALU.mult).then_inc(hid_done, 1)

            def hidden_low(b, j, k):
                dve.wait_ge(hhi_done, b * HC + j + 1)
                nc.vector.tensor_tensor(cols(h_lo, j * S, S), hid[:, k, :], cols(h_hi, j * S, S),
                                        ALU.subtract).then_inc(hlo_done, 1)

            def w2_scale(n, c):
                if c >= 2:
                    dve.wait_ge(w2_lo_done, n * 4 + (c - 1))
                nc.vector.tensor_scalar(stage[:, c % 2, :], cols(w2_f32, (n * 4 + c) * D, D),
                                        cols(rowmul, n * 4 + c, 1), None, ALU.mult).then_inc(w2_scaled, 1)

            def w2_low(n, c):
                dve.wait_ge(w2_hi_done, n * 4 + (c + 1))
                flat = w2r[:].rearrange("p c s n -> p (c s n)")
                at = (n * 4 + c) * 2 * D
                nc.vector.tensor_tensor(flat[:, bass.ds(at + D, D)], stage[:, c % 2, :], flat[:, bass.ds(at, D)],
                                        ALU.subtract).then_inc(w2_lo_done, 1)

            def weight_scales():
                dve.wait_ge(w_scaled, 2 * HC)
                bits(sc13[:], tb13[:], 1, 50 * ONE)
                dve.wait_ge(dve_step, step.next())
                pair = sc13[:].rearrange("p (j w) -> p w j", w=2)
                nc.vector.tensor_tensor(rowmul[:], pair[:, 0, :], pair[:, 1, :], ALU.mult).then_inc(dve_step, 1)
                dve.wait_ge(dve_step, step.next())
                dve.wait_ge(sq_done, HC)
                nc.vector.tensor_reduce(peaks[:, 0:1], sq2[:], AX_X, ALU.max).then_inc(dve_step, 1)
                dve.wait_ge(dve_step, step.next())
                nc.vector.tensor_reduce(peaks[:, 1:2], rowmul[:], AX_X, ALU.max).then_inc(peaks_done, 1)
                dve.wait_ge(gpeaks_done, 1)
                nc.vector.tensor_scalar(gs[:, 0:1].bitcast(I32), gpeaks[:, 0:1].bitcast(I32), 24, 23,
                                        ALU.logical_shift_right, ALU.logical_shift_left).then_inc(dve_step, 1)
                dve.wait_ge(dve_step, step.next())
                bits(gs[:, 1:2], gs[:, 0:1], -1, 198 * ONE)
                bits(gs[:, 2:3], gs[:, 0:1], 1, 50 * ONE)
                bits(gs[:, 3:4], gpeaks[:, 1:2], -1, 254 * ONE)
                step.next()
                step.next()
                dve.wait_ge(dve_step, step.next())
                nc.vector.tensor_scalar(rowmul[:], rowmul[:], gs[:, 3:4], gs[:, 1:2], ALU.mult,
                                        ALU.mult).then_inc(dve_step, 1)
                nc.vector.tensor_scalar(outmul[:], gpeaks[:, 1:2], 2.0 ** 30 / float(H) ** 0.5, gs[:, 2:3], ALU.mult,
                                        ALU.mult).then_inc(dve_step, 1)
                step.next()
                dve.wait_ge(dve_step, step.next())
                dve.wait_ge(fly_done, KC)

            def gate_phase(b, weights, following):
                def chunk(j, k, prep, q, convert):
                    if prep:
                        scale_w13(j + AHEAD, k)
                    if q is not None:
                        u, i, s = q
                        if s is not None:
                            for n in range(TI):
                                dve.wait_ge(ctx_in[n], b * 16 + 32)
                            context_max(b + 1, i, s)
                        quantise(b + 1, u, i, u_par(u, k), s, True)
                    if convert is not None:
                        w2_scale(convert, 0)
                        w2_scale(convert, 1)
                    hidden(b, j, k)
                    if prep:
                        low_w13(j + AHEAD)
                    if convert is not None:
                        w2_low(convert, 0)
                        w2_low(convert, 1)
                        w2_scale(convert, 2)
                        w2_scale(convert, 3)
                        w2_low(convert, 2)
                        w2_low(convert, 3)
                        dve.wait_ge(w2_lo_done, convert * 4 + 4)
                    hidden_low(b, j, k)

                def u_par(u, k):
                    return (k + 1) % 2

                p = 4 * weights
                q0 = Q_FROM - 1
                gate_steps(dve, 0, q0, lambda j, k, n: chunk(j, k, weights, None, None))
                if following:
                    x_stats(b + 1, (0, 1))
                    gate_steps(dve, q0, q0 + TI, lambda j, k, n: chunk(j, k, weights, (n, n, (k + 1) % 2), None),
                               step, 2 * (p + 5))
                    x_stats(b + 1, (2, 3))
                    inverse_root(mv1[:, :, 1], rs1[:], TI)
                    gate_steps(dve, q0 + TI, q0 + NQ, lambda j, k, n: chunk(j, k, weights, (n + TI, n, None), None),
                               step, 2 * (p + 8))
                else:
                    gate_steps(dve, q0, q0 + NQ, lambda j, k, n: chunk(j, k, weights, None, None), step, 2 * p)
                gate_steps(dve, q0 + NQ, Q_FROM + NQ, lambda j, k, n: chunk(j, k, weights, None, None))
                if following:
                    block_scales()
                if weights:
                    weight_scales()
                gate_steps(dve, Q_FROM + NQ, HC, lambda j, k, n: chunk(j, k, False, None, n if weights else None),
                           step, 0)

            def down_phase(b, following):
                def tile(i, k):
                    if following:
                        add_products(b + 1, i, lambda kb: ps_x[:, kb % 2, :])
                        row_stats(x_tile(b + 1, i), mv2[:, k, :])
                        inverse_root(mv2[:, k, 1:2], rs2[:, k:k + 1], 1)
                        normalise(b + 1, i, k, mv2[:, k, 0:1], rs2[:, k:k + 1])
                    dve.wait_ge(down_ready, b * TI + i + 1)
                    y = x_tile(b, i)
                    nc.vector.scalar_tensor_tensor(out=y, in0=ps_d[:, k, :], scalar=outmul[:, 0:1], in1=y,
                                                   op0=ALU.mult, op1=ALU.add).then_inc(out_ready, 1)

                with dve.Fori(0, TI // 2) as r:
                    with step.loop(r, TI // 2, 2 * ((TI - 1) * KC + 2 + 12) * following):
                        for k in range(2):
                            tile(r * 2 + k, k)

            for n, freed in enumerate((silu_done, hid_done, hlo_done, out_ready)):
                nc.vector.memset(credit[:, n:n + 1], 0.0).then_inc(freed, 2)

            context_max(0, 0, 0)
            for i in range(TI):
                if i + 1 < TI:
                    context_max(0, i + 1, i + 1)
                quantise(0, i, i, i % 2, i, i >= 2)
            x_stats(0, range(TI))
            inverse_root(mv1[:, :, 1], rs1[:], TI)
            for i in range(TI):
                quantise(0, TI + i, i, i % 2, None, True)
            block_scales()
            for j in range(AHEAD):
                scale_w13(j, j % 2)
                low_w13(j)
            for i in range(TI):
                add_products(0, i, lambda kb: (ps_g if kb < 2 else ps_u)[:, kb % 2, :])
                row_stats(x_tile(0, i), mv2[:, i, :])
            inverse_root(mv2[:, :, 1], rs2[:], TI)
            for i in range(TI):
                normalise(0, i, i % 2, mv2[:, i, 0:1], rs2[:, i:i + 1])
            gate_phase(0, True, True)
            down_phase(0, True)
            with dve.Fori(1, NB - 1) as b:
                with step.loop(b - 1, NB - 2, 4 + TI * 5 + 4 + 12 + TI * 8 + 1 + TI * ((TI - 1) * KC + 2 + 12)):
                    gate_phase(b, False, True)
                    down_phase(b, True)
            gate_phase(NB - 1, False, False)
            down_phase(NB - 1, False)


_INS = ["x", "ctx_2048", "L0_ffn_W1", "L0_ffn_W2", "L0_ffn_W3"]


def kernel(**inputs):
    import numpy as _np
    import concourse.bacc as _bacc
    from concourse import mybir as _mybir
    from concourse.bass_utils import run_bass_kernel_spmd as _run

    nc = _bacc.Bacc("TRN2", target_bir_lowering=False, num_devices=1)
    i = _np.arange(128)
    odd = _np.array([[bin(a & b).count("1") % 2 for b in i] for a in i])
    consts = {
        "eye32": _np.eye(128, dtype=_np.float32),
        "eye16": _np.eye(128, dtype=_np.float16),
        "had": (1 - 2 * odd).astype(_np.float32),
    }
    arrays, aps = {}, {}
    for name, a in [(n, _np.ascontiguousarray(inputs[n])) for n in _INS] + list(consts.items()):
        arrays[f"in_{name}_dram"] = a
        aps[name] = nc.dram_tensor(f"in_{name}_dram", a.shape, _mybir.dt.from_np(a.dtype), kind="ExternalInput").ap()
    shape = inputs["x"].shape
    out = nc.dram_tensor("out_0_dram", shape, _mybir.dt.float32, kind="ExternalOutput").ap()
    xattn_ffn(nc, aps["x"], aps["ctx_2048"], aps["L0_ffn_W1"], aps["L0_ffn_W2"], aps["L0_ffn_W3"],
              aps["eye32"], aps["eye16"], aps["had"], out)
    r = _run(nc, [arrays], core_ids=[0])
    return r.results[0]["out_0_dram"]
```

```python
from contextlib import ExitStack, contextmanager

import concourse.bass as bass
from concourse import mybir

F32 = mybir.dt.float32
F16 = mybir.dt.float16
I32 = mybir.dt.int32
ALU = mybir.AluOpType
ACT = mybir.ActivationFunctionType
AX_X = mybir.AxisListType.X
RMAX = bass.bass_isa.ReduceOp.max

P = 128
FP8_MAX = 448.0
ACT_EPS, W_EPS, LN_EPS = 1e-4, 1e-6, 1e-5
EXPONENT = 0x7F800000
ONE = 1 << 23
ROUNDER = 1.5 * 2.0 ** 20
LEAST_NORMAL = 2.0 ** -6
Z_SCALE = 2.0 ** 11


class Count:

    def __init__(self):
        self.base, self.n = 0, 0

    def next(self):
        self.n += 1
        return self.base + self.n

    @contextmanager
    def loop(self, index, trips, each):
        base, n = self.base, self.n
        self.base, self.n = base + index * each + n, 0
        yield
        assert self.n == each, f"{self.n} steps a trip, not {each}"
        self.base, self.n = base, n + trips * each


def cols(t, start, n):
    return t[:, bass.ds(start, n)]


def blocks(ap):
    return ap.rearrange("p (k n) -> p k n", n=P)


def xattn_ffn(nc, x, ctx_w, w1, w2, w3, eye32_in, eye16_in, had_in, out):
    NB, S, D = x.shape
    H = w1.shape[0]
    KC = D // P
    TI = S // P
    HC = H // P
    assert D == 512 and S == 512 and KC == 4 and TI == 4 and HC == 16 and NB >= 3
    SLOTS = 4
    AHEAD = 5
    Q_FROM = 4
    NQ = 2 * TI
    G_FROM = 11
    PRODUCTS_AT = (4, 5, 7, 9)
    UNIT_AT = (1, 2, 4, 5, 9, 10, 12, 13)

    x_rows = x.rearrange("b s d -> (b s) d")
    ctx_rows = ctx_w.rearrange("b s d -> (b s) d")
    out_rows = out.rearrange("b s d -> (b s) d")

    with ExitStack() as stack:
        def sb(name, shape, dt):
            return stack.enter_context(nc.sbuf_tensor(name, shape, dt))

        def sem(name):
            return stack.enter_context(nc.semaphore(name))

        w13_hi = sb("w13_hi", [P, 2, KC, H], F16)
        w13_lo = sb("w13_lo", [P, 2, KC, H], F16)
        w2r = sb("w2r", [P, HC, 2, D], F16)
        w2_f32 = w2r[:].rearrange("p c s n -> p (c s n)").bitcast(F32)
        w2_f32c = w2_f32.rearrange("p (c n) -> p c n", c=HC)
        h_hi = sb("h_hi", [P, HC * S], F16)
        h_lo = sb("h_lo", [P, HC * S], F16)
        zt_hi = sb("zt_hi", [P, KC, S], F16)
        zt_lo = sb("zt_lo", [P, KC, S], F16)
        qt_ctx = sb("qt_ctx", [P, KC, S], F16)
        qt_x = sb("qt_x", [P, KC, S], F16)
        x_sb = sb("x_sb", [P, 2 * TI * D], F32)
        ctx_sb = sb("ctx_sb", [P, TI * D], F32)
        zb = sb("zb", [P, 2, D], F32)
        mb = sb("mb", [P, 2, D], F32)
        qb = sb("qb", [P, 2, D], F16)
        z_hl = sb("z_hl", [P, 2, D], F16)
        hid = sb("hid", [P, 2, S], F32)
        ring = sb("ring", [P, SLOTS, D], F32)
        stage = sb("stage", [P, 2, D], F32)
        fly = sb("fly", [P, HC, P], F32)
        junk = sb("junk", [P, D], F16)
        eye32 = sb("eye32", [P, P], F32)
        eye16 = sb("eye16", [P, P], F16)
        had = sb("had", [P, P], F32)
        bn = sb("bn", [P, 6], F32)
        mv1 = sb("mv1", [P, TI, 2], F32)
        mv2 = sb("mv2", [P, TI, 2], F32)
        rs1 = sb("rs1", [P, TI], F32)
        rs2 = sb("rs2", [P, TI], F32)
        ve = sb("ve", [P, TI], F32)
        half = sb("half", [P, TI], F32)
        camax = sb("camax", [P, TI, KC], F32)
        cmax = sb("cmax", [P, TI, KC], F32)
        xamax = sb("xamax", [P, KC], F32)
        safe = sb("safe", [P, KC], F32)
        rq = sb("rq", [P, KC], F32)
        sx = sb("sx", [P, TI * KC], F32)
        sw = sb("sw", [P, TI * KC], F32)
        coef = sb("coef", [P, TI * KC * TI], F32)
        sq13 = sb("sq13", [P, HC * 2], F32)
        tb13 = sb("tb13", [P, HC * 2], F32)
        sc13 = sb("sc13", [P, HC * 2], F32)
        silu_sc = sb("silu_sc", [P, HC], F32)
        hid_sc = sb("hid_sc", [P, HC], F32)
        sq2 = sb("sq2", [P, HC], F32)
        rowmul = sb("rowmul", [P, HC], F32)
        peaks = sb("peaks", [P, 2], F32)
        gpeaks = sb("gpeaks", [P, 2], F32)
        gs = sb("gs", [P, 4], F32)
        outmul = sb("outmul", [P, 1], F32)
        credit = sb("credit", [P, 4], F32)

        ps_g = stack.enter_context(nc.psum_tensor("ps_g", [P, 2, 512], F32))
        ps_u = stack.enter_context(nc.psum_tensor("ps_u", [P, 2, 512], F32))
        ps_d = stack.enter_context(nc.psum_tensor("ps_d", [P, 2, 512], F32))
        ps_x = stack.enter_context(nc.psum_tensor("ps_x", [P, 2, 512], F32))

        passed = sem("passed")
        const_in = sem("const_in")
        ctx_in = [sem(f"ctx_in{i}") for i in range(TI)]
        x_in = [sem(f"x_in{i}") for i in range(TI)]
        w_in = [sem(f"w_in{i}") for i in range(SLOTS)]
        y_out = [sem(f"y_out{i}") for i in range(TI)]
        dve_step = sem("dve_step")
        camax_done = sem("camax_done")
        ctx_read = sem("ctx_read")
        v_done = sem("v_done")
        g_used = sem("g_used")
        zn_done = sem("zn_done")
        zlo_done = sem("zlo_done")
        out_ready = sem("out_ready")
        var_done = sem("var_done")
        sc13_done = sem("sc13_done")
        w13_lo_done = sem("w13_lo_done")
        hid_done = sem("hid_done")
        hlo_done = sem("hlo_done")
        peaks_done = sem("peaks_done")
        w2_scaled = sem("w2_scaled")
        w2_lo_done = sem("w2_lo_done")
        sq_done = sem("sq_done")
        w2_staged = sem("w2_staged")
        w2_stored = sem("w2_stored")
        w_scaled = sem("w_scaled")
        w13_hi_done = sem("w13_hi_done")
        silu_done = sem("silu_done")
        hhi_done = sem("hhi_done")
        q_stored = sem("q_stored")
        zhi_done = sem("zhi_done")
        zt_stored = sem("zt_stored")
        w2_hi_done = sem("w2_hi_done")
        w2_turned = sem("w2_turned")
        w2_mixed = sem("w2_mixed")
        w13_turned = sem("w13_turned")
        gate_ready = sem("gate_ready")
        up_ready = sem("up_ready")
        q_turned = sem("q_turned")
        g_ready = sem("g_ready")
        z_turned = sem("z_turned")
        down_ready = sem("down_ready")
        pool_step = sem("pool_step")
        cmax_done = sem("cmax_done")
        q_done = sem("q_done")
        root_done = sem("root_done")
        fly_done = sem("fly_done")
        gpeaks_done = sem("gpeaks_done")

        def alone(eng):
            eng.sem_inc(passed, 1)

        def par(b):
            return b % 2

        def x_tile(b, i):
            return cols(x_sb, (par(b) * TI + i) * D, D)

        def d_bank(i):
            return ps_d[:].rearrange("p k n -> p (k n)")[:, bass.ds(i % 2 * 512, 512)]

        def gate_steps(eng, j0, j1, body, counter=None, each=0):
            trips = (j1 - j0) // 2
            if trips > 1:
                with eng.Fori(0, trips) as r, (counter or Count()).loop(r, trips, 2 * each):
                    for k in range(2):
                        body(j0 + k + r * 2, (j0 + k) % 2, k + r * 2)
            for j in range(j0 + 2 * trips if trips > 1 else j0, j1):
                body(j, j % 2, j - j0)

        def root_event(b, i):
            if isinstance(b, int) and b == 0:
                return 0 if i is None else 1
            return (b - 1) * (TI + 1) + 2 + (0 if i is None else i + 1)

        block = stack.enter_context(nc.Block())

        @block.sync
        def _(sp):
            def load_batch(b):
                for i in range(TI):
                    if not (isinstance(b, int) and b == 0):
                        sp.wait_ge(ctx_read, b * TI + i + 1 - TI)
                        alone(sp)
                        sp.wait_ge(ctx_in[i], b * 16)
                        alone(sp)
                    sp.dma_start(cols(ctx_sb, i * D, D),
                                 ctx_rows[bass.ds(b * S + i * P, P), :]).then_inc(ctx_in[i], 16)
                for i in range(TI):
                    if not (isinstance(b, int) and b == 0):
                        sp.wait_ge(x_in[i], b * 16)
                        alone(sp)
                        if not (isinstance(b, int) and b == 1):
                            sp.wait_ge(y_out[i], b * 16 - 16)
                        alone(sp)
                    sp.dma_start(x_tile(b, i), x_rows[bass.ds(b * S + i * P, P), :]).then_inc(x_in[i], 16)

            def store_batch(b):
                for i in range(TI):
                    sp.wait_ge(out_ready, b * TI + (i + 1) + 2)
                    sp.dma_start(out_rows[bass.ds(b * S + i * P, P), :], x_tile(b, i)).then_inc(y_out[i], 16)

            def load_w2(dc, hq, wait):
                if wait:
                    sp.wait_ge(w2_turned, dc * 4 + hq - SLOTS + 1)
                    sp.wait_ge(sq_done, dc * 4 + hq - SLOTS + 1)
                sp.dma_start(ring[:, hq, :], w2[bass.ds(dc * P, P), hq * 512:(hq + 1) * 512]).then_inc(w_in[hq], 16)

            def load_w13(j, k, wait):
                for w, src in enumerate((w1, w3)):
                    slot = 2 * k + w
                    if wait:
                        sp.wait_ge(w13_turned, j * 2 + w - SLOTS + 1)
                    sp.dma_start(ring[:, slot, :], src[bass.ds(j * P, P), :]).then_inc(w_in[slot], 16)

            load_batch(0)
            sp.dma_start(eye32[:], eye32_in).then_inc(const_in, 16)
            sp.dma_start(eye16[:], eye16_in).then_inc(const_in, 16)
            sp.dma_start(had[:], had_in).then_inc(const_in, 16)
            for hq in range(4):
                load_w2(0, hq, False)
            with sp.Fori(1, KC) as dc:
                for hq in range(4):
                    load_w2(dc, hq, True)
            for j in range(2):
                for w in range(2):
                    sp.wait_ge(w2_turned, 4 * KC - SLOTS + 2 * j + w + 1)
                    sp.wait_ge(sq_done, 4 * KC - SLOTS + 2 * j + w + 1)
                load_w13(j, j, False)
            load_batch(1)
            with sp.Fori(1, HC // 2) as r:
                for k in range(2):
                    load_w13(r * 2 + k, k, True)
            store_batch(0)
            with sp.Fori(1, NB - 1) as b:
                load_batch(b + 1)
                store_batch(b)
            store_batch(NB - 1)
            for i in range(TI):
                sp.wait_ge(y_out[i], 16 * NB)

        @block.tensor
        def _(pe):
            def turn_w2(t, hq):
                pe.wait_ge(w_in[hq], t // 4 * 16 + 16)
                if t > 0:
                    pe.wait_ge(w2_staged, t)
                for k in range(4):
                    last = nc.tensor.transpose(ps_d[:, 0, k * P:(k + 1) * P],
                                               ring[:, hq, k * P:(k + 1) * P], eye32[:])
                last.then_inc(w2_turned, 1)

            def mix_w2(t):
                pe.wait_ge(w2_staged, t + 1)
                if t > 0:
                    pe.wait_ge(w2_stored, t)
                nc.tensor.matmul(ps_d[:, 1, :], had[:], stage[:, t % 2, :],
                                 start=True, stop=True).then_inc(w2_mixed, 1)

            def turn_w13(j, k, first=False):
                for w in range(2):
                    pe.wait_ge(w_scaled, j * 2 + w + 1)
                    if first:
                        pe.wait_ge(w2_stored, HC)
                    else:
                        pe.wait_ge(w13_lo_done, j * 2 + (w - 1))
                    for c in range(KC):
                        last = nc.tensor.transpose(ps_d[:, w, c * P:(c + 1) * P],
                                                   ring[:, 2 * k + w, c * P:(c + 1) * P], eye32[:])
                    last.then_inc(w13_turned, 1)

            def turn_q(b, u, k, free):
                pe.wait_ge(q_done, b * NQ + u + 1)
                if free is not None:
                    pe.wait_ge(*free)
                for c in range(KC):
                    last = nc.tensor.transpose(ps_x[:, k, 0:D // 2].bitcast(F16)[:, c * P:(c + 1) * P],
                                               qb[:, k, c * P:(c + 1) * P], eye16[:])
                last.then_inc(q_turned, 1)

            def block_product(b, i, kb, bank):
                nc.tensor.matmul(bank, qt_x[:, kb, bass.ds(i * P, P)], qt_ctx[:, kb, :],
                                 start=True, stop=True).then_inc(g_ready, 1)

            def turn_z(b, i, free):
                pe.wait_ge(zlo_done, b * TI + i + 1)
                if free is not None:
                    pe.wait_ge(*free)
                for s in range(2):
                    for c in range(KC):
                        last = nc.tensor.transpose(ps_x[:, s, 0:D // 2].bitcast(F16)[:, c * P:(c + 1) * P],
                                                   z_hl[:, s, c * P:(c + 1) * P], eye16[:])
                last.then_inc(z_turned, 1)

            def project(bank, w, j, done):
                n = 0
                for c in range(KC):
                    for wt, zt in ((w13_hi, zt_hi), (w13_hi, zt_lo), (w13_lo, zt_hi)):
                        last = nc.tensor.matmul(bank, wt[:, w, c, bass.ds(j * P, P)], zt[:, c, :],
                                                start=n == 0, stop=n == 3 * KC - 1)
                        n += 1
                last.then_inc(done, 1)

            def gate_phase(b, weights, following):
                pe.wait_ge(zt_stored, b * TI + TI)
                alone(pe)

                def chunk(j, k, prep, unit, product):
                    pe.wait_ge(silu_done, b * HC + j + 1)
                    project(ps_g[:, k, :], 0, j, gate_ready)
                    if prep:
                        turn_w13(j + AHEAD, (k + AHEAD) % 2)
                    if product is not None:
                        n, bank = product
                        pe.wait_ge(q_stored, (b + 1) * NQ + NQ - 1 + bank)
                        pe.wait_ge(g_used, (b + 1) * TI * KC + n - 1)
                        block_product(b + 1, 0, n, ps_x[:, bank, :])
                    pe.wait_ge(hid_done, b * HC + j + 1)
                    project(ps_u[:, k, :], 1, j, up_ready)
                    if unit is not None:
                        turn_q(b + 1, unit, k, (q_stored, (b + 1) * NQ + unit - 1))

                f = following
                gate_steps(pe, 0, Q_FROM, lambda j, k, n: chunk(j, k, weights, None, None))
                gate_steps(pe, Q_FROM, G_FROM, lambda j, k, n: chunk(j, k, weights, n if f else None, None))
                if f:
                    chunk(G_FROM, G_FROM % 2, False, NQ - 1, (0, 0))
                    gate_steps(pe, G_FROM + 1, G_FROM + KC,
                               lambda j, k, n: chunk(j, k, False, None, (n + 1, (k + 1) % 2)))
                    chunk(HC - 1, (HC - 1) % 2, False, None, None)
                else:
                    gate_steps(pe, G_FROM, HC, lambda j, k, n: chunk(j, k, False, None, None))

            def down_phase(b, first, following):
                if first:
                    pe.wait_ge(w13_lo_done, 2 * HC)

                def tile(i, last_tile):
                    pe.wait_ge(out_ready, b * TI + i + 1)
                    n = 0
                    for c in range(HC):
                        pe.wait_ge(hlo_done, b * HC + (c + 1) + 2)
                        if first:
                            pe.wait_ge(w2_lo_done, c + 1)
                        for ht, s in ((h_hi, 0), (h_hi, 1), (h_lo, 0)):
                            last = nc.tensor.matmul(d_bank(i), ht[:, bass.ds(i * P + c * S, P)], w2r[:, c, s, :],
                                                    start=n == 0, stop=n == 3 * HC - 1)
                            n += 1
                        if following and c == 1:
                            turn_z(b + 1, i, None)
                        if following and not last_tile and c in PRODUCTS_AT:
                            kb = PRODUCTS_AT.index(c)
                            g = (b + 1) * TI * KC + i * KC + (KC + kb)
                            if kb < 2:
                                pe.wait_ge(zt_stored, (b + 1) * TI + i + 1)
                            else:
                                pe.wait_ge(g_used, g - 1)
                            block_product(b + 1, i + 1, kb, ps_x[:, kb % 2, :])
                    last.then_inc(down_ready, 1)

                with pe.Fori(0, TI - 1) as i:
                    tile(i, False)
                tile(TI - 1, True)

            pe.wait_ge(const_in, 48)
            for t in range(HC):
                turn_w2(t, t % 4)
                if t:
                    mix_w2(t - 1)
                if t in UNIT_AT:
                    u = UNIT_AT.index(t)
                    turn_q(0, u, u % 2, (q_stored, u - 1) if u >= 2 else None)
            mix_w2(HC - 1)
            pe.wait_ge(q_stored, NQ)

            def first_products(i):
                for kb in range(KC):
                    g = i * KC + kb
                    if g >= 4:
                        pe.wait_ge(g_used, g - 3)
                    block_product(0, i, kb, (ps_g if kb < 2 else ps_u)[:, kb % 2, :])

            first_products(0)
            for i in range(1, TI):
                first_products(i)
                turn_w13(i - 1, (i - 1) % 2, first=i == 1)
            for i in range(TI):
                turn_z(0, i, (zt_stored, i) if i else None)
            for j in range(TI - 1, AHEAD):
                turn_w13(j, j % 2)
            pe.wait_ge(g_used, TI * KC)
            gate_phase(0, True, True)
            down_phase(0, True, True)
            with pe.Fori(1, NB - 1) as b:
                gate_phase(b, False, True)
                down_phase(b, False, True)
            gate_phase(NB - 1, False, False)
            down_phase(NB - 1, False, False)

        @block.scalar
        def _(act):
            def store_q(b, u, k, dst, i):
                act.wait_ge(q_turned, b * NQ + u + 1)
                nc.scalar.copy(dst[:, :, bass.ds(i * P, P)],
                               blocks(ps_x[:, k, 0:D // 2].bitcast(F16))).then_inc(q_stored, 1)

            def split_w13(j):
                for w in range(2):
                    act.wait_ge(w13_turned, j * 2 + w + 1)
                    nc.scalar.copy(w13_hi[:, w, :, bass.ds(j * P, P)], blocks(ps_d[:, w, :])).then_inc(w13_hi_done, 1)

            def norm_w13(j, k):
                for w in range(2):
                    slot = 2 * k + w
                    act.wait_ge(w_in[slot], (KC + 1) * 16 + (j - k) * 8)
                    act.wait_ge(sq_done, j * 2 + (w + HC))
                    nc.scalar.activation(junk[:], ring[:, slot, :], ACT.Square,
                                         accum_out=cols(sq13, j * 2 + w, 1)).then_inc(sq_done, 1)

            def scale_w13(j, k):
                act.wait_ge(sc13_done, j + 1)
                for w in range(2):
                    tile = ring[:, 2 * k + w, :]
                    nc.scalar.mul(tile, tile, cols(sc13, j * 2 + w, 1)).then_inc(w_scaled, 1)

            def z_high(b, i, k):
                act.wait_ge(zn_done, b * TI + i + 1)
                if not (isinstance(b, int) and b == 0 and isinstance(i, int) and i == 0):
                    act.wait_ge(z_turned, b * TI + i)
                nc.scalar.mul(z_hl[:, 0, :], zb[:, k, :], Z_SCALE).then_inc(zhi_done, 1)

            def store_z(b, i):
                act.wait_ge(z_turned, b * TI + i + 1)
                for s, dst in enumerate((zt_hi, zt_lo)):
                    last = nc.scalar.copy(dst[:, :, bass.ds(i * P, P)], blocks(ps_x[:, s, 0:D // 2].bitcast(F16)))
                last.then_inc(zt_stored, 1)

            def gate_phase(b, weights, following):
                def chunk(j, k, prep, q, convert):
                    s = (k + AHEAD) % 2
                    if prep:
                        scale_w13(j + AHEAD, s)
                        if prep > 1:
                            norm_w13(j + (AHEAD + 1), 1 - s)
                    if convert is not None:
                        convert_high(convert, 0)
                    act.wait_ge(gate_ready, b * HC + j + 1)
                    act.wait_ge(hlo_done, b * HC + j + 1)
                    nc.scalar.activation(hid[:, k, :], ps_g[:, k, :], ACT.Silu,
                                         scale=cols(silu_sc, j, 1)).then_inc(silu_done, 1)
                    if prep:
                        split_w13(j + AHEAD)
                    if convert is not None:
                        convert_high(convert, 2)
                    act.wait_ge(hid_done, b * HC + (j + 1) + 2)
                    nc.scalar.copy(cols(h_hi, j * S, S), hid[:, k, :]).then_inc(hhi_done, 1)
                    if q is not None:
                        u, dst, i = q
                        store_q(b + 1, u, k, dst, i)

                def convert_high(n, c0):
                    for c in range(c0, c0 + 2):
                        act.wait_ge(w2_scaled, n * 4 + (c + 1))
                        nc.scalar.copy(w2r[:].rearrange("p c s n -> p (c s n)")[:, bass.ds((n * 4 + c) * 2 * D, D)],
                                       stage[:, c % 2, :]).then_inc(w2_hi_done, 1)

                both, one = (2, 1) if weights else (0, 0)
                f = following

                def q_of(n):
                    return (n, qt_ctx, n) if f else None

                def q_of_x(n):
                    return (n + TI, qt_x, n) if f else None

                gate_steps(act, 0, Q_FROM, lambda j, k, n: chunk(j, k, both, None, None))
                gate_steps(act, Q_FROM, Q_FROM + TI, lambda j, k, n: chunk(j, k, both, q_of(n), None))
                gate_steps(act, Q_FROM + TI, G_FROM - 1, lambda j, k, n: chunk(j, k, both, q_of_x(n), None))
                chunk(G_FROM - 1, (G_FROM - 1) % 2, one, q_of_x(TI - 2), None)
                chunk(G_FROM, G_FROM % 2, False, q_of_x(TI - 1), 0 if weights else None)
                gate_steps(act, G_FROM + 1, HC - 1,
                           lambda j, k, n: chunk(j, k, False, None, n + 1 if weights else None))
                chunk(HC - 1, (HC - 1) % 2, False, None, None)

            def down_phase(b):
                z_high(b + 1, 0, 0)
                with act.Fori(0, TI - 1) as i:
                    store_z(b + 1, i)
                    z_high(b + 1, i + 1, 0)
                store_z(b + 1, TI - 1)

            for t in range(HC):
                dc, hq = t // 4, t % 4
                act.wait_ge(w_in[hq], dc * 16 + 16)
                if t:
                    act.wait_ge(sq_done, t)
                nc.scalar.activation(junk[:], ring[:, hq, :], ACT.Square,
                                     accum_out=sq2[:, t:t + 1]).then_inc(sq_done, 1)
                act.wait_ge(w2_turned, t + 1)
                if t >= 2:
                    act.wait_ge(w2_mixed, t - 1)
                nc.scalar.copy(stage[:, t % 2, :], ps_d[:, 0, :]).then_inc(w2_staged, 1)
                if t:
                    s = t - 1
                    act.wait_ge(w2_mixed, s + 1)
                    nc.scalar.copy(w2_f32c[:, 4 * (s % 4):4 * (s % 4) + 4, (s // 4) * P:(s // 4 + 1) * P],
                                   blocks(ps_d[:, 1, :])).then_inc(w2_stored, 1)
                if t in UNIT_AT:
                    u = UNIT_AT.index(t)
                    store_q(0, u, u % 2, qt_ctx if u < TI else qt_x, u % TI)
            act.wait_ge(w2_mixed, HC)
            nc.scalar.copy(w2_f32c[:, HC - 4:HC, (KC - 1) * P:KC * P], blocks(ps_d[:, 1, :])).then_inc(w2_stored, 1)
            norm_w13(0, 0)

            def first_w13(j):
                scale_w13(j, j % 2)
                norm_w13(j + 1, (j + 1) % 2)
                split_w13(j)

            for j in range(TI - 1):
                first_w13(j)
            for i in range(TI):
                z_high(0, i, i % 2)
                store_z(0, i)
            for j in range(TI - 1, AHEAD):
                first_w13(j)
            gate_phase(0, True, True)
            down_phase(0)
            with act.Fori(1, NB - 1) as b:
                gate_phase(b, False, True)
                down_phase(b)
            gate_phase(NB - 1, False, False)

        @block.gpsimd
        def _(pool):
            step = Count()

            def block_max(b, i, s):
                pool.wait_ge(camax_done, b * TI + i + 1)
                alone(pool)
                nc.gpsimd.partition_all_reduce(cmax[:, s, :], camax[:, s, :], P, RMAX).then_inc(cmax_done, 1)

            def round_tile(b, u, k):
                pool.wait_ge(v_done, b * NQ + u + 1)
                nc.gpsimd.tensor_tensor(zb[:, k, :], zb[:, k, :], mb[:, k, :], ALU.add).then_inc(pool_step, 1)
                if not (isinstance(b, int) and b == 0 and u < 2):
                    pool.wait_ge(q_turned, b * NQ + u - 1)
                pool.wait_ge(pool_step, step.next())
                nc.gpsimd.tensor_tensor(qb[:, k, :], zb[:, k, :], mb[:, k, :], ALU.subtract).then_inc(q_done, 1)

            def butterfly(dc, n):
                stride, op = 1 << (n // 2), (ALU.add, ALU.subtract)[n % 2]
                a = w2_f32c[:, :, dc * P:(dc + 1) * P]
                src, dst = (a, fly[:]) if n // 2 % 2 == 0 else (fly[:], a)
                sv = src.rearrange("p (a t r) d -> p a t r d", t=2, r=stride)
                dv = dst.rearrange("p (a t r) d -> p a t r d", t=2, r=stride)
                if n == 0:
                    pool.wait_ge(w2_stored, 4 * dc + 4)
                    if dc:
                        pool.wait_ge(fly_done, dc)
                elif n % 2 == 0:
                    pool.wait_ge(pool_step, step.base + step.n)
                if stride == 1:
                    o, x0, x1 = dv[:, :, n % 2, 0, :], sv[:, :, 0, 0, :], sv[:, :, 1, 0, :]
                elif stride == 8:
                    o, x0, x1 = dv[:, 0, n % 2, :, :], sv[:, 0, 0, :, :], sv[:, 0, 1, :, :]
                else:
                    o, x0, x1 = dv[:, :, n % 2, :, :], sv[:, :, 0, :, :], sv[:, :, 1, :, :]
                last = nc.gpsimd.tensor_tensor(o, x0, x1, op)
                if n < 7:
                    last.then_inc(pool_step, 1)
                    step.next()
                else:
                    last.then_inc(fly_done, 1)

            def inverse_root(event, root):
                pool.wait_ge(var_done, event + 1)
                n = root.shape[1]
                nc.gpsimd.tensor_tensor(root, ve[:, 0:n], half[:, 0:n], ALU.pow).then_inc(root_done, 1)

            nc.gpsimd.memset(half[:], -0.5).then_inc(pool_step, 1)
            pool.wait_ge(pool_step, step.next())
            block_max(0, 0, 0)
            for i in range(1, TI):
                block_max(0, i, i)
                round_tile(0, i - 1, (i - 1) % 2)
            inverse_root(root_event(0, None), rs1[:])
            for u in range(TI - 1, NQ):
                round_tile(0, u, u % 2)
            for n in range(8):
                butterfly(0, n)
            inverse_root(root_event(0, 0), rs2[:])
            for n in range(8):
                butterfly(1, n)
            inverse_root(root_event(1, None), rs1[:])
            for u in range(NQ):
                if u < TI:
                    block_max(1, u, u % 2)
                round_tile(1, u, u % 2)
                butterfly(2 + u // 4, 2 * (u % 4))
                butterfly(2 + u // 4, 2 * (u % 4) + 1)
            pool.wait_ge(peaks_done, 1)
            nc.gpsimd.partition_all_reduce(gpeaks[:], peaks[:], P, RMAX).then_inc(gpeaks_done, 1)
            for i in range(TI):
                inverse_root(root_event(1, i), rs2[:, 0:1])
            with pool.Fori(2, NB) as b:
                inverse_root(root_event(b, None), rs1[:])
                with step.loop(b - 2, NB - 2, NQ):
                    for u0 in (0, TI):
                        with pool.Fori(0, TI // 2) as r, step.loop(r, TI // 2, 2):
                            for k in range(2):
                                if u0 == 0:
                                    block_max(b, r * 2 + k, k)
                                round_tile(b, r * 2 + (u0 + k), k)
                for i in range(TI):
                    inverse_root(root_event(b, i), rs2[:, 0:1])

        @block.vector
        def _(dve):
            step = Count()

            def variance(var):
                nc.vector.tensor_scalar(ve[:, 0:var.shape[1]], var, LN_EPS, None, ALU.add).then_inc(var_done, 1)

            def row_stats(src, mv):
                alone(dve)
                nc.vector.bn_stats(bn[:], src).then_inc(dve_step, 1)
                dve.wait_ge(dve_step, step.next())
                alone(dve)
                nc.vector.bn_aggr(mv, bn[:]).then_inc(dve_step, 1)
                dve.wait_ge(dve_step, step.next())
                alone(dve)

            def x_stats(b, tiles):
                for i in tiles:
                    dve.wait_ge(x_in[i], b * 16 + 16)
                    row_stats(x_tile(b, i), mv1[:, i, :])

            def context_max(b, i, s):
                if isinstance(i, int):
                    dve.wait_ge(ctx_in[i], b * 16 + 16)
                nc.vector.tensor_reduce(camax[:, s, :], blocks(cols(ctx_sb, i * D, D)), AX_X, ALU.max,
                                        apply_absolute_value=True).then_inc(camax_done, 1)

            def quantise(b, u, i, k, s, free):
                context = s is not None
                src = cols(ctx_sb, i * D, D) if context else x_tile(b, i)
                eps, scales = (W_EPS, sw) if context else (ACT_EPS, sx)
                z = zb[:, k, :]
                if free:
                    dve.wait_ge(q_done, b * NQ + u - 1)
                if context:
                    dve.wait_ge(cmax_done, b * TI + i + 1)
                    peak = cmax[:, s, :]
                else:
                    nc.vector.tensor_scalar(z, src, mv1[:, :, 0:1].rearrange("p a b -> p (a b)")[:, bass.ds(i, 1)],
                                            cols(rs1, i, 1), ALU.subtract, ALU.mult).then_inc(dve_step, 1)
                    dve.wait_ge(dve_step, step.next())
                    src, peak = z, xamax[:]
                    nc.vector.tensor_reduce(peak, blocks(z), AX_X, ALU.max,
                                            apply_absolute_value=True).then_inc(dve_step, 1)
                    dve.wait_ge(dve_step, step.next())
                nc.vector.tensor_scalar(safe[:], peak, eps, None, ALU.max).then_inc(dve_step, 1)
                dve.wait_ge(dve_step, step.next())
                nc.vector.reciprocal(rq[:], safe[:]).then_inc(dve_step, 1)
                nc.vector.tensor_scalar(cols(scales, i * KC, KC), safe[:], 1.0 / FP8_MAX, None,
                                        ALU.mult).then_inc(dve_step, 1)
                step.next()
                dve.wait_ge(dve_step, step.next())
                nc.vector.tensor_scalar(rq[:], rq[:], FP8_MAX, None, ALU.mult).then_inc(dve_step, 1)
                dve.wait_ge(dve_step, step.next())
                scaled = nc.vector.tensor_tensor(blocks(z), blocks(src), rq[:].unsqueeze(2).broadcast_to([P, KC, P]),
                                                 ALU.mult)
                if context:
                    scaled.then_inc(ctx_read, 1)
                    dve.wait_ge(ctx_read, b * TI + i + 1)
                else:
                    scaled.then_inc(dve_step, 1)
                    dve.wait_ge(dve_step, step.next())
                nc.vector.tensor_scalar(mb[:, k, :].bitcast(I32), z.bitcast(I32), EXPONENT, None,
                                        ALU.bitwise_and).then_inc(dve_step, 1)
                dve.wait_ge(dve_step, step.next())
                nc.vector.tensor_scalar(mb[:, k, :], mb[:, k, :], LEAST_NORMAL, ROUNDER, ALU.max,
                                        ALU.mult).then_inc(v_done, 1)

            def block_scales():
                shape = [P, TI, KC, TI]
                a = sx[:].rearrange("p (i k) -> p i k", i=TI).unsqueeze(3).broadcast_to(shape)
                w = sw[:].rearrange("p (n k) -> p k n", n=TI).unsqueeze(1).broadcast_to(shape)
                nc.vector.tensor_tensor(coef[:].rearrange("p (i k n) -> p i k n", i=TI, k=KC), a, w,
                                        ALU.mult).then_inc(dve_step, 1)
                dve.wait_ge(dve_step, step.next())
                alone(dve)

            def add_product(b, i, kb, bank):
                g = (b * TI + i) * KC + kb
                dve.wait_ge(g_ready, g + 1)
                if not isinstance(g, int) or g > 0:
                    dve.wait_ge(g_used, g)
                for nb in range(TI):
                    y = cols(x_sb, (par(b) * TI + i) * D + nb * P, P)
                    last = nc.vector.scalar_tensor_tensor(
                        out=y, in0=bank[:, nb * P:(nb + 1) * P], scalar=cols(coef, (i * KC + kb) * TI + nb, 1),
                        in1=y, op0=ALU.mult, op1=ALU.add)
                last.then_inc(g_used, 1)

            def y_stats(b, i, mv):
                dve.wait_ge(g_used, (b * TI + i) * KC + KC)
                row_stats(x_tile(b, i), mv)

            def normalise(b, i, k, mv, root, free):
                if free is not None:
                    dve.wait_ge(zlo_done, free)
                nc.vector.tensor_scalar(zb[:, k, :], x_tile(b, i), mv, root, ALU.subtract,
                                        ALU.mult).then_inc(zn_done, 1)

            def z_low(b, i, k):
                dve.wait_ge(zhi_done, b * TI + i + 1)
                dve.wait_ge(zn_done, b * TI + i + 1)
                nc.vector.scalar_tensor_tensor(out=z_hl[:, 1, :], in0=zb[:, k, :], scalar=Z_SCALE, in1=z_hl[:, 0, :],
                                               op0=ALU.mult, op1=ALU.subtract).then_inc(zlo_done, 1)

            def bits(dst, src, n, m, done):
                nc.vector.tensor_scalar(dst.bitcast(I32), src.bitcast(I32), float(n), float(m), ALU.mult,
                                        ALU.add).then_inc(done, 1)

            def scales_w13(j):
                dve.wait_ge(sq_done, j * 2 + (2 + HC))
                t = cols(tb13, j * 2, 2)
                nc.vector.tensor_scalar(t.bitcast(I32), cols(sq13, j * 2, 2).bitcast(I32), 24, 23,
                                        ALU.logical_shift_right, ALU.logical_shift_left).then_inc(dve_step, 1)
                dve.wait_ge(dve_step, step.next())
                bits(cols(silu_sc, j, 1), cols(tb13, j * 2, 1), 1, 39 * ONE, dve_step)
                bits(cols(hid_sc, j, 1), cols(tb13, j * 2, 1), -1, 169 * ONE, dve_step)
                step.next()
                step.next()
                bits(cols(sc13, j * 2, 2), t, -1, 204 * ONE, sc13_done)

            def low_w13(j):
                for w in range(2):
                    dve.wait_ge(w13_hi_done, j * 2 + w + 1)
                    at = (slice(None), w, slice(None), bass.ds(j * P, P))
                    nc.vector.tensor_tensor(w13_lo[at], blocks(ps_d[:, w, :]), w13_hi[at],
                                            ALU.subtract).then_inc(w13_lo_done, 1)

            def hidden(b, j, k):
                dve.wait_ge(silu_done, b * HC + (j + 1) + 2)
                dve.wait_ge(up_ready, b * HC + j + 1)
                nc.vector.scalar_tensor_tensor(out=hid[:, k, :], in0=hid[:, k, :], scalar=cols(hid_sc, j, 1),
                                               in1=ps_u[:, k, :], op0=ALU.mult, op1=ALU.mult).then_inc(hid_done, 1)

            def hidden_low(b, j, k):
                dve.wait_ge(hhi_done, b * HC + j + 1)
                nc.vector.tensor_tensor(cols(h_lo, j * S, S), hid[:, k, :], cols(h_hi, j * S, S),
                                        ALU.subtract).then_inc(hlo_done, 1)

            def w2_scale(n, c):
                if c >= 2:
                    dve.wait_ge(w2_lo_done, n * 4 + (c - 1))
                nc.vector.tensor_scalar(stage[:, c % 2, :], cols(w2_f32, (n * 4 + c) * D, D),
                                        cols(rowmul, n * 4 + c, 1), None, ALU.mult).then_inc(w2_scaled, 1)

            def w2_low(n, c):
                dve.wait_ge(w2_hi_done, n * 4 + (c + 1))
                flat = w2r[:].rearrange("p c s n -> p (c s n)")
                at = (n * 4 + c) * 2 * D
                nc.vector.tensor_tensor(flat[:, bass.ds(at + D, D)], stage[:, c % 2, :], flat[:, bass.ds(at, D)],
                                        ALU.subtract).then_inc(w2_lo_done, 1)

            def weight_scales():
                dve.wait_ge(w_scaled, 2 * HC)
                bits(sc13[:], tb13[:], 1, 50 * ONE, dve_step)
                dve.wait_ge(dve_step, step.next())
                pair = sc13[:].rearrange("p (j w) -> p w j", w=2)
                nc.vector.tensor_tensor(rowmul[:], pair[:, 0, :], pair[:, 1, :], ALU.mult).then_inc(dve_step, 1)
                dve.wait_ge(dve_step, step.next())
                dve.wait_ge(sq_done, HC)
                nc.vector.tensor_reduce(peaks[:, 0:1], sq2[:], AX_X, ALU.max).then_inc(dve_step, 1)
                dve.wait_ge(dve_step, step.next())
                nc.vector.tensor_reduce(peaks[:, 1:2], rowmul[:], AX_X, ALU.max).then_inc(peaks_done, 1)
                dve.wait_ge(gpeaks_done, 1)
                nc.vector.tensor_scalar(gs[:, 0:1].bitcast(I32), gpeaks[:, 0:1].bitcast(I32), 24, 23,
                                        ALU.logical_shift_right, ALU.logical_shift_left).then_inc(dve_step, 1)
                dve.wait_ge(dve_step, step.next())
                bits(gs[:, 1:2], gs[:, 0:1], -1, 198 * ONE, dve_step)
                bits(gs[:, 2:3], gs[:, 0:1], 1, 50 * ONE, dve_step)
                bits(gs[:, 3:4], gpeaks[:, 1:2], -1, 254 * ONE, dve_step)
                step.next()
                step.next()
                dve.wait_ge(dve_step, step.next())
                nc.vector.tensor_scalar(rowmul[:], rowmul[:], gs[:, 3:4], gs[:, 1:2], ALU.mult,
                                        ALU.mult).then_inc(dve_step, 1)
                nc.vector.tensor_scalar(outmul[:], gpeaks[:, 1:2], 2.0 ** 30 / float(H) ** 0.5, gs[:, 2:3], ALU.mult,
                                        ALU.mult).then_inc(dve_step, 1)
                step.next()
                dve.wait_ge(dve_step, step.next())
                dve.wait_ge(fly_done, KC)

            def gate_phase(b, weights, following):
                def chunk(j, k, prep, q, convert, product):
                    if q is not None:
                        u, i, s = q
                        if s is not None:
                            for n in range(TI):
                                dve.wait_ge(ctx_in[n], b * 16 + 32)
                            context_max(b + 1, i, s)
                        quantise(b + 1, u, i, (k + 1) % 2, s, True)
                    if prep > 1:
                        scales_w13(j + (AHEAD + 1))
                    if convert is not None:
                        w2_scale(convert, 0)
                        w2_scale(convert, 1)
                    if product is not None:
                        n, bank = product
                        add_product(b + 1, 0, n, ps_x[:, bank, :])
                    hidden(b, j, k)
                    if prep:
                        low_w13(j + AHEAD)
                    if convert is not None:
                        w2_low(convert, 0)
                        w2_low(convert, 1)
                        w2_scale(convert, 2)
                        w2_scale(convert, 3)
                        w2_low(convert, 2)
                        w2_low(convert, 3)
                        dve.wait_ge(w2_lo_done, convert * 4 + 4)
                    hidden_low(b, j, k)

                both, one = (2, 1) if weights else (0, 0)
                f = following
                p = 3 * weights
                q0 = Q_FROM - 1
                chunk(0, 0, both, None, None, None)
                chunk(1, 1, both, None, None, None)
                if f:
                    x_stats(b + 1, (0, 1))
                chunk(2, 0, both, None, None, None)
                if f:
                    x_stats(b + 1, (2, 3))
                    variance(mv1[:, :, 1])
                gate_steps(dve, q0, q0 + TI, lambda j, k, n: chunk(j, k, both, (n, n, (k + 1) % 2) if f else None,
                                                                   None, None), step, p + 5 * f)
                if f:
                    dve.wait_ge(root_done, root_event(b + 1, None) + 1)
                    alone(dve)

                def x_of(n):
                    return (n + TI, n, None) if f else None

                gate_steps(dve, q0 + TI, q0 + NQ - 1, lambda j, k, n: chunk(j, k, both, x_of(n), None, None),
                           step, p + 8 * f)
                chunk(q0 + NQ - 1, (q0 + NQ - 1) % 2, one, x_of(TI - 1), None, None)
                if f:
                    block_scales()
                if weights:
                    weight_scales()
                gate_steps(dve, G_FROM, G_FROM + KC,
                           lambda j, k, n: chunk(j, k, False, None, n if weights else None,
                                                 (n, (k + 1) % 2) if f else None))
                if f:
                    y_stats(b + 1, 0, mv2[:, 0, :])
                    variance(mv2[:, 0, 1:2])
                chunk(HC - 1, (HC - 1) % 2, False, None, None, None)

            def down_phase(b, following):
                def z_of(i):
                    dve.wait_ge(root_done, root_event(b + 1, i) + 1)
                    normalise(b + 1, i, 0, mv2[:, 0, 0:1], rs2[:, 0:1], (b + 1) * TI + i)
                    z_low(b + 1, i, 0)

                def store(i):
                    dve.wait_ge(down_ready, b * TI + i + 1)
                    y = x_tile(b, i)
                    nc.vector.scalar_tensor_tensor(out=y, in0=d_bank(i), scalar=outmul[:, 0:1], in1=y,
                                                   op0=ALU.mult, op1=ALU.add).then_inc(out_ready, 1)

                if following:
                    z_of(0)
                with dve.Fori(0, TI - 1) as i, step.loop(i, TI - 1, 2 * following):
                    if following:
                        for kb in range(KC):
                            add_product(b + 1, i + 1, kb, ps_x[:, kb % 2, :])
                        y_stats(b + 1, i + 1, mv2[:, 0, :])
                        variance(mv2[:, 0, 1:2])
                        z_of(i + 1)
                    store(i)
                store(TI - 1)

            for n, freed in enumerate((silu_done, hid_done, hlo_done, out_ready)):
                nc.vector.memset(credit[:, n:n + 1], 0.0).then_inc(freed, 2)

            context_max(0, 0, 0)
            for i in range(TI):
                if i + 1 < TI:
                    context_max(0, i + 1, i + 1)
                quantise(0, i, i, i % 2, i, i >= 2)
                if i == TI - 2:
                    x_stats(0, range(TI))
                    variance(mv1[:, :, 1])
            dve.wait_ge(root_done, root_event(0, None) + 1)
            for i in range(TI):
                quantise(0, TI + i, i, i % 2, None, True)
            block_scales()
            for i in range(TI):
                for kb in range(KC):
                    add_product(0, i, kb, (ps_g if kb < 2 else ps_u)[:, kb % 2, :])
                scales_w13(i)
                if i:
                    low_w13(i - 1)
                y_stats(0, i, mv2[:, i, :])
            variance(mv2[:, :, 1])
            dve.wait_ge(root_done, root_event(0, 0) + 1)
            for i in range(TI):
                normalise(0, i, i % 2, mv2[:, i, 0:1], rs2[:, i:i + 1], i - 1 if i > 1 else None)
                z_low(0, i, i % 2)
            for j in range(TI - 1, AHEAD):
                scales_w13(j + 1)
                low_w13(j)
            gate_phase(0, True, True)
            down_phase(0, True)
            with dve.Fori(1, NB - 1) as b:
                with step.loop(b - 1, NB - 2, TI * 2 + TI * 5 + TI * 8 + 1 + TI * 2):
                    gate_phase(b, False, True)
                    down_phase(b, True)
            gate_phase(NB - 1, False, False)
            down_phase(NB - 1, False)


_INS = ["x", "ctx_2048", "L0_ffn_W1", "L0_ffn_W2", "L0_ffn_W3"]


def kernel(**inputs):
    import numpy as _np
    import concourse.bacc as _bacc
    from concourse import mybir as _mybir
    from concourse.bass_utils import run_bass_kernel_spmd as _run

    nc = _bacc.Bacc("TRN2", target_bir_lowering=False, num_devices=1)
    i = _np.arange(128)
    odd = _np.array([[bin(a & b).count("1") % 2 for b in i] for a in i])
    consts = {
        "eye32": _np.eye(128, dtype=_np.float32),
        "eye16": _np.eye(128, dtype=_np.float16),
        "had": (1 - 2 * odd).astype(_np.float32),
    }
    arrays, aps = {}, {}
    for name, a in [(n, _np.ascontiguousarray(inputs[n])) for n in _INS] + list(consts.items()):
        arrays[f"in_{name}_dram"] = a
        aps[name] = nc.dram_tensor(f"in_{name}_dram", a.shape, _mybir.dt.from_np(a.dtype), kind="ExternalInput").ap()
    shape = inputs["x"].shape
    out = nc.dram_tensor("out_0_dram", shape, _mybir.dt.float32, kind="ExternalOutput").ap()
    xattn_ffn(nc, aps["x"], aps["ctx_2048"], aps["L0_ffn_W1"], aps["L0_ffn_W2"], aps["L0_ffn_W3"],
              aps["eye32"], aps["eye16"], aps["had"], out)
    r = _run(nc, [arrays], core_ids=[0])
    return r.results[0]["out_0_dram"]
```

```python
from contextlib import ExitStack, contextmanager

import concourse.bass as bass
from concourse import mybir

F32 = mybir.dt.float32
F16 = mybir.dt.float16
I32 = mybir.dt.int32
ALU = mybir.AluOpType
ACT = mybir.ActivationFunctionType
AX_X = mybir.AxisListType.X
RMAX = bass.bass_isa.ReduceOp.max

P = 128
FP8_MAX = 448.0
ACT_EPS, W_EPS, LN_EPS = 1e-4, 1e-6, 1e-5
EXPONENT = 0x7F800000
ONE = 1 << 23
ROUNDER = 1.5 * 2.0 ** 20
LEAST_NORMAL = 2.0 ** -6
Z_SCALE = 2.0 ** 11


class Count:

    def __init__(self):
        self.base, self.n = 0, 0

    def next(self):
        self.n += 1
        return self.base + self.n

    @contextmanager
    def loop(self, index, trips, each):
        base, n = self.base, self.n
        self.base, self.n = base + index * each + n, 0
        yield
        assert self.n == each, f"{self.n} steps a trip, not {each}"
        self.base, self.n = base, n + trips * each


def cols(t, start, n):
    return t[:, bass.ds(start, n)]


def blocks(ap):
    return ap.rearrange("p (k n) -> p k n", n=P)


def xattn_ffn(nc, x, ctx_w, w1, w2, w3, eye32_in, eye16_in, had_in, out):
    NB, S, D = x.shape
    H = w1.shape[0]
    KC = D // P
    TI = S // P
    HC = H // P
    assert D == 512 and S == 512 and KC == 4 and TI == 4 and HC == 16 and NB >= 3
    SLOTS = 4
    AHEAD = 4
    Q_FROM = 4
    NQ = 2 * TI
    FLY_ROOTS, FLY_MAX, FLY_X, FLY_UNITS = (2, 3, 3, 3), 3, 6, (1, 1, 1, 1, 2, 2, 2, 2)
    W2_SPLIT = (4, 4, 2, 6)
    G_FROM = 11
    PRODUCTS_AT = (4, 5, 8, 9)
    TURN_AT = 2
    UNIT_AT = (1, 2, 4, 5, 8, 9, 11, 12)
    G_AT = (10, 13)

    x_rows = x.rearrange("b s d -> (b s) d")
    ctx_rows = ctx_w.rearrange("b s d -> (b s) d")
    out_rows = out.rearrange("b s d -> (b s) d")

    with ExitStack() as stack:
        def sb(name, shape, dt):
            return stack.enter_context(nc.sbuf_tensor(name, shape, dt))

        def sem(name):
            return stack.enter_context(nc.semaphore(name))

        w13_hi = sb("w13_hi", [P, 2, KC, H], F16)
        w13_lo = sb("w13_lo", [P, 2, KC, H], F16)
        w2r = sb("w2r", [P, HC, 2, D], F16)
        w2_f32 = w2r[:].rearrange("p c s n -> p (c s n)").bitcast(F32)
        w2_f32c = w2_f32.rearrange("p (c n) -> p c n", c=HC)
        h_hi = sb("h_hi", [P, HC * S], F16)
        h_lo = sb("h_lo", [P, HC * S], F16)
        zt_hi = sb("zt_hi", [P, KC, S], F16)
        zt_lo = sb("zt_lo", [P, KC, S], F16)
        qt_ctx = sb("qt_ctx", [P, KC, S], F16)
        qt_x = sb("qt_x", [P, KC, S], F16)
        x_sb = sb("x_sb", [P, 2 * TI * D], F32)
        ctx_sb = sb("ctx_sb", [P, TI * D], F32)
        zb = sb("zb", [P, 2, D], F32)
        mb = sb("mb", [P, 2, D], F32)
        qb = sb("qb", [P, 2, D], F16)
        z_hl = sb("z_hl", [P, 2, D], F16)
        hid = sb("hid", [P, 2, S], F32)
        ring = sb("ring", [P, SLOTS, D], F32)
        stage = sb("stage", [P, 2, D], F32)
        fly = sb("fly", [P, HC, P], F32)
        junk = cols(h_hi, (HC - 1) * S, D)
        eye32 = sb("eye32", [P, P], F32)
        eye16 = sb("eye16", [P, P], F16)
        had = sb("had", [P, P], F32)
        bn = sb("bn", [P, TI, 6], F32)
        mv1 = sb("mv1", [P, TI, 2], F32)
        mv2 = sb("mv2", [P, TI, 2], F32)
        rs1 = sb("rs1", [P, TI], F32)
        rs2 = sb("rs2", [P, TI], F32)
        ve = sb("ve", [P, TI], F32)
        half = sb("half", [P, TI], F32)
        camax = sb("camax", [P, TI * KC], F32)
        cmax = sb("cmax", [P, TI * KC], F32)
        xamax = sb("xamax", [P, KC], F32)
        safe = sb("safe", [P, KC], F32)
        rq = sb("rq", [P, KC], F32)
        sx = sb("sx", [P, TI * KC], F32)
        sw = sb("sw", [P, TI * KC], F32)
        coef = sb("coef", [P, TI * KC * TI], F32)
        sq13 = sb("sq13", [P, HC * 2], F32)
        tb13 = sb("tb13", [P, HC * 2], F32)
        sc13 = sb("sc13", [P, HC * 2], F32)
        silu_sc = sb("silu_sc", [P, HC], F32)
        hid_sc = sb("hid_sc", [P, HC], F32)
        sq2 = sb("sq2", [P, HC], F32)
        rowmul = sb("rowmul", [P, HC], F32)
        peaks = sb("peaks", [P, 2], F32)
        gpeaks = sb("gpeaks", [P, 2], F32)
        gs = sb("gs", [P, 4], F32)
        outmul = sb("outmul", [P, 1], F32)
        credit = sb("credit", [P, 4], F32)

        ps_g = stack.enter_context(nc.psum_tensor("ps_g", [P, 2, 512], F32))
        ps_u = stack.enter_context(nc.psum_tensor("ps_u", [P, 2, 512], F32))
        ps_d = stack.enter_context(nc.psum_tensor("ps_d", [P, 2, 512], F32))
        ps_x = stack.enter_context(nc.psum_tensor("ps_x", [P, 2, 512], F32))

        passed = sem("passed")
        const_in = sem("const_in")
        ctx_in = [sem(f"ctx_in{i}") for i in range(TI)]
        x_in = [sem(f"x_in{i}") for i in range(TI)]
        w_in = [sem(f"w_in{i}") for i in range(SLOTS)]
        y_out = [sem(f"y_out{i}") for i in range(TI)]
        dve_step = sem("dve_step")
        camax_done = sem("camax_done")
        ctx_read = sem("ctx_read")
        v_done = sem("v_done")
        g_half_used = sem("g_half_used")
        g_used = sem("g_used")
        zn_done = sem("zn_done")
        zlo_done = sem("zlo_done")
        out_ready = sem("out_ready")
        var_done = sem("var_done")
        sc13_done = sem("sc13_done")
        w13_lo_done = sem("w13_lo_done")
        hid_done = sem("hid_done")
        hlo_done = sem("hlo_done")
        peaks_done = sem("peaks_done")
        rowmul_done = sem("rowmul_done")
        w2_lo_done = sem("w2_lo_done")
        sq_done = sem("sq_done")
        w2_staged = sem("w2_staged")
        w2_stored = sem("w2_stored")
        w_scaled = sem("w_scaled")
        w13_hi_done = sem("w13_hi_done")
        silu_done = sem("silu_done")
        hhi_done = sem("hhi_done")
        q_stored = sem("q_stored")
        zhi_done = sem("zhi_done")
        zt_stored = sem("zt_stored")
        w2_hi_done = sem("w2_hi_done")
        w2_turned = sem("w2_turned")
        w2_mixed = sem("w2_mixed")
        w13_turned = sem("w13_turned")
        gate_ready = sem("gate_ready")
        up_ready = sem("up_ready")
        q_turned = sem("q_turned")
        g_ready = sem("g_ready")
        z_turned = sem("z_turned")
        down_ready = sem("down_ready")
        pool_step = sem("pool_step")
        cmax_done = sem("cmax_done")
        q_done = sem("q_done")
        root_done = sem("root_done")
        fly_done = sem("fly_done")
        gpeaks_done = sem("gpeaks_done")
        w2_scaled = sem("w2_scaled")

        def alone(eng):
            eng.sem_inc(passed, 1)

        def par(b):
            return b % 2

        def x_tile(b, i):
            return cols(x_sb, (par(b) * TI + i) * D, D)

        def d_bank(i):
            return ps_d[:].rearrange("p k n -> p (k n)")[:, bass.ds(i % 2 * 512, 512)]

        def gate_steps(eng, j0, j1, body, counter=None, each=0):
            trips = (j1 - j0) // 2
            if trips > 1:
                with eng.Fori(0, trips) as r, (counter or Count()).loop(r, trips, 2 * each):
                    for k in range(2):
                        body(j0 + k + r * 2, (j0 + k) % 2, k + r * 2)
            for j in range(j0 + 2 * trips if trips > 1 else j0, j1):
                body(j, j % 2, j - j0)

        def root_event(b, i):
            return b * (TI + 1) + (0 if i is None else i + 1)

        block = stack.enter_context(nc.Block())

        @block.sync
        def _(sp):
            def load_batch(b):
                for i in range(TI):
                    if not (isinstance(b, int) and b == 0):
                        sp.wait_ge(ctx_read, b * TI + i + 1 - TI)
                        alone(sp)
                        sp.wait_ge(ctx_in[i], b * 16)
                        alone(sp)
                    sp.dma_start(cols(ctx_sb, i * D, D),
                                 ctx_rows[bass.ds(b * S + i * P, P), :]).then_inc(ctx_in[i], 16)
                for i in range(TI):
                    if not (isinstance(b, int) and b == 0):
                        sp.wait_ge(x_in[i], b * 16)
                        alone(sp)
                        if not (isinstance(b, int) and b == 1):
                            sp.wait_ge(y_out[i], b * 16 - 16)
                        alone(sp)
                    sp.dma_start(x_tile(b, i), x_rows[bass.ds(b * S + i * P, P), :]).then_inc(x_in[i], 16)

            def store_batch(b):
                for i in range(TI):
                    sp.wait_ge(out_ready, b * TI + (i + 1) + 2)
                    sp.dma_start(out_rows[bass.ds(b * S + i * P, P), :], x_tile(b, i)).then_inc(y_out[i], 16)

            def load_w2(dc, hq, wait):
                if wait:
                    sp.wait_ge(w2_turned, dc * 4 + hq - SLOTS + 1)
                    sp.wait_ge(sq_done, dc * 4 + hq - SLOTS + 1)
                sp.dma_start(ring[:, hq, :], w2[bass.ds(dc * P, P), hq * 512:(hq + 1) * 512]).then_inc(w_in[hq], 16)

            def load_w13(j, k, wait):
                for w, src in enumerate((w1, w3)):
                    slot = 2 * k + w
                    if wait:
                        sp.wait_ge(w13_turned, j * 2 + w - SLOTS + 1)
                    sp.dma_start(ring[:, slot, :], src[bass.ds(j * P, P), :]).then_inc(w_in[slot], 16)

            load_batch(0)
            sp.dma_start(eye32[:], eye32_in).then_inc(const_in, 16)
            sp.dma_start(eye16[:], eye16_in).then_inc(const_in, 16)
            sp.dma_start(had[:], had_in).then_inc(const_in, 16)
            for hq in range(4):
                load_w2(0, hq, False)
            with sp.Fori(1, KC) as dc:
                for hq in range(4):
                    load_w2(dc, hq, True)
            for j in range(2):
                for w in range(2):
                    sp.wait_ge(w2_turned, 4 * KC - SLOTS + 2 * j + w + 1)
                    sp.wait_ge(sq_done, 4 * KC - SLOTS + 2 * j + w + 1)
                load_w13(j, j, False)
            load_batch(1)
            with sp.Fori(1, HC // 2) as r:
                for k in range(2):
                    load_w13(r * 2 + k, k, True)
            store_batch(0)
            with sp.Fori(1, NB - 1) as b:
                load_batch(b + 1)
                store_batch(b)
            store_batch(NB - 1)
            for i in range(TI):
                sp.wait_ge(y_out[i], 16 * NB)

        @block.tensor
        def _(pe):
            def turn_w2(t, hq):
                pe.wait_ge(w_in[hq], t // 4 * 16 + 16)
                if t > 0:
                    pe.wait_ge(w2_staged, t)
                for k in range(4):
                    last = nc.tensor.transpose(ps_d[:, 0, k * P:(k + 1) * P],
                                               ring[:, hq, k * P:(k + 1) * P], eye32[:])
                last.then_inc(w2_turned, 1)

            def mix_w2(t):
                pe.wait_ge(w2_staged, t + 1)
                if t > 0:
                    pe.wait_ge(w2_stored, t)
                nc.tensor.matmul(ps_d[:, 1, :], had[:], stage[:, t % 2, :],
                                 start=True, stop=True).then_inc(w2_mixed, 1)

            def turn_w13(j, k, first=False):
                for w in range(2):
                    pe.wait_ge(w_scaled, j * 2 + w + 1)
                    if first:
                        pe.wait_ge(w2_stored, HC)
                    else:
                        pe.wait_ge(w13_lo_done, j * 2 + (w - 1))
                    for c in range(KC):
                        last = nc.tensor.transpose(ps_d[:, w, c * P:(c + 1) * P],
                                                   ring[:, 2 * k + w, c * P:(c + 1) * P], eye32[:])
                    last.then_inc(w13_turned, 1)

            def turn_q(b, u, k, free):
                pe.wait_ge(q_done, b * NQ + u + 1)
                if free is not None:
                    pe.wait_ge(*free)
                for c in range(KC):
                    last = nc.tensor.transpose(ps_x[:, k, 0:D // 2].bitcast(F16)[:, c * P:(c + 1) * P],
                                               qb[:, k, c * P:(c + 1) * P], eye16[:])
                last.then_inc(q_turned, 1)

            def block_product(b, i, kb, bank):
                nc.tensor.matmul(bank, qt_x[:, kb, bass.ds(i * P, P)], qt_ctx[:, kb, :],
                                 start=True, stop=True).then_inc(g_ready, 1)

            def turn_z(b, i, free):
                pe.wait_ge(zlo_done, b * TI + i + 1)
                if free is not None:
                    pe.wait_ge(*free)
                for s in range(2):
                    for c in range(KC):
                        last = nc.tensor.transpose(ps_x[:, s, 0:D // 2].bitcast(F16)[:, c * P:(c + 1) * P],
                                                   z_hl[:, s, c * P:(c + 1) * P], eye16[:])
                last.then_inc(z_turned, 1)

            def project(bank, w, j, done):
                n = 0
                for c in range(KC):
                    for wt, zt in ((w13_hi, zt_hi), (w13_hi, zt_lo), (w13_lo, zt_hi)):
                        last = nc.tensor.matmul(bank, wt[:, w, c, bass.ds(j * P, P)], zt[:, c, :],
                                                start=n == 0, stop=n == 3 * KC - 1)
                        n += 1
                last.then_inc(done, 1)

            def gate_phase(b, weights, following):
                pe.wait_ge(zt_stored, b * TI + TI)
                alone(pe)

                def chunk(j, k, prep, unit, product):
                    pe.wait_ge(silu_done, b * HC + j + 1)
                    project(ps_g[:, k, :], 0, j, gate_ready)
                    if product is not None:
                        n, bank = product
                        pe.wait_ge(q_stored, (b + 1) * NQ + NQ - 1 + bank)
                        pe.wait_ge(g_used, (b + 1) * TI * KC + n - 1)
                        block_product(b + 1, 0, n, ps_x[:, bank, :])
                    pe.wait_ge(hid_done, b * HC + j + 1)
                    project(ps_u[:, k, :], 1, j, up_ready)
                    if unit is not None:
                        turn_q(b + 1, unit, k, (q_stored, (b + 1) * NQ + unit - 1))
                    if prep:
                        turn_w13(j + AHEAD, (k + AHEAD) % 2)

                f = following
                gate_steps(pe, 0, Q_FROM, lambda j, k, n: chunk(j, k, weights, None, None))
                gate_steps(pe, Q_FROM, G_FROM, lambda j, k, n: chunk(j, k, weights, n if f else None, None))
                if f:
                    chunk(G_FROM, G_FROM % 2, weights, NQ - 1, (0, 0))
                    gate_steps(pe, G_FROM + 1, G_FROM + KC,
                               lambda j, k, n: chunk(j, k, False, None, (n + 1, (k + 1) % 2)))
                    chunk(HC - 1, (HC - 1) % 2, False, None, None)
                else:
                    gate_steps(pe, G_FROM, HC, lambda j, k, n: chunk(j, k, False, None, None))

            def down_phase(b, first, following):
                if first:
                    pe.wait_ge(w13_lo_done, 2 * HC)

                def tile(i, last_tile):
                    pe.wait_ge(out_ready, b * TI + i + 1)
                    n = 0
                    for c in range(HC):
                        pe.wait_ge(hlo_done, b * HC + (c + 1) + 2)
                        if first:
                            pe.wait_ge(w2_lo_done, c + 1)
                        for ht, s in ((h_hi, 0), (h_hi, 1), (h_lo, 0)):
                            last = nc.tensor.matmul(d_bank(i), ht[:, bass.ds(i * P + c * S, P)], w2r[:, c, s, :],
                                                    start=n == 0, stop=n == 3 * HC - 1)
                            n += 1
                        if following and c == TURN_AT:
                            turn_z(b + 1, i, None)
                        if following and not last_tile and c in PRODUCTS_AT:
                            kb = PRODUCTS_AT.index(c)
                            g = (b + 1) * TI * KC + i * KC + (KC + kb)
                            if kb < 2:
                                pe.wait_ge(zt_stored, (b + 1) * TI + i + 1)
                            else:
                                pe.wait_ge(g_used, g - 1)
                            block_product(b + 1, i + 1, kb, ps_x[:, kb % 2, :])
                    last.then_inc(down_ready, 1)

                with pe.Fori(0, TI - 1) as i:
                    tile(i, False)
                tile(TI - 1, True)

            pe.wait_ge(const_in, 48)
            def step_w2(t):
                turn_w2(t, t % 4)
                if t:
                    mix_w2(t - 1)

            def first_products(i):
                for kb in range(KC):
                    g = i * KC + kb
                    if g >= 4:
                        pe.wait_ge(g_used, g - 3)
                    block_product(0, i, kb, (ps_g if kb < 2 else ps_u)[:, kb % 2, :])

            for t in range(HC):
                step_w2(t)
                if t in UNIT_AT:
                    u = UNIT_AT.index(t)
                    turn_q(0, u, u % 2, (q_stored, u - 1) if u >= 2 else None)
                if t in G_AT:
                    pe.wait_ge(q_stored, TI + G_AT.index(t) + 1)
                    first_products(G_AT.index(t))
            mix_w2(HC - 1)
            pe.wait_ge(q_stored, NQ)
            for i in range(TI):
                if i + 2 < TI:
                    first_products(i + 2)
                turn_z(0, i, (zt_stored, i) if i else None)
                turn_w13(i, i % 2, first=i == 0)
            pe.wait_ge(g_used, TI * KC)
            gate_phase(0, True, True)
            down_phase(0, True, True)
            with pe.Fori(1, NB - 1) as b:
                gate_phase(b, False, True)
                down_phase(b, False, True)
            gate_phase(NB - 1, False, False)
            down_phase(NB - 1, False, False)

        @block.scalar
        def _(act):
            def store_q(b, u, k, dst, i):
                act.wait_ge(q_turned, b * NQ + u + 1)
                nc.scalar.copy(dst[:, :, bass.ds(i * P, P)],
                               blocks(ps_x[:, k, 0:D // 2].bitcast(F16))).then_inc(q_stored, 1)

            def split_w13(j):
                for w in range(2):
                    act.wait_ge(w13_turned, j * 2 + w + 1)
                    nc.scalar.copy(w13_hi[:, w, :, bass.ds(j * P, P)], blocks(ps_d[:, w, :])).then_inc(w13_hi_done, 1)

            def norm_w13(j, k):
                for w in range(2):
                    slot = 2 * k + w
                    act.wait_ge(w_in[slot], (KC + 1) * 16 + (j - k) * 8)
                    act.wait_ge(sq_done, j * 2 + (w + HC))
                    nc.scalar.activation(junk, ring[:, slot, :], ACT.Square,
                                         accum_out=cols(sq13, j * 2 + w, 1)).then_inc(sq_done, 1)

            def scale_w13(j, k):
                act.wait_ge(sc13_done, j + 1)
                for w in range(2):
                    tile = ring[:, 2 * k + w, :]
                    nc.scalar.mul(tile, tile, cols(sc13, j * 2 + w, 1)).then_inc(w_scaled, 1)

            def z_high(b, i, k):
                act.wait_ge(zn_done, b * TI + i + 1)
                if not (isinstance(b, int) and b == 0 and isinstance(i, int) and i == 0):
                    act.wait_ge(z_turned, b * TI + i)
                nc.scalar.mul(z_hl[:, 0, :], zb[:, k, :], Z_SCALE).then_inc(zhi_done, 1)

            def store_z(b, i):
                act.wait_ge(z_turned, b * TI + i + 1)
                for s, dst in enumerate((zt_hi, zt_lo)):
                    last = nc.scalar.copy(dst[:, :, bass.ds(i * P, P)], blocks(ps_x[:, s, 0:D // 2].bitcast(F16)))
                last.then_inc(zt_stored, 1)

            def gate_phase(b, weights, following):
                def chunk(j, k, prep, q, z0=False):
                    s = (k + AHEAD + 1) % 2
                    act.wait_ge(gate_ready, b * HC + j + 1)
                    act.wait_ge(hlo_done, b * HC + j + 1)
                    nc.scalar.activation(hid[:, k, :], ps_g[:, k, :], ACT.Silu,
                                         scale=cols(silu_sc, j, 1)).then_inc(silu_done, 1)
                    if prep > 1:
                        norm_w13(j + (AHEAD + 1), s)
                    if z0:
                        z_high(b + 1, 0, 0)
                    act.wait_ge(hid_done, b * HC + (j + 1) + 2)
                    nc.scalar.copy(cols(h_hi, j * S, S), hid[:, k, :]).then_inc(hhi_done, 1)
                    if q is not None:
                        u, dst, i = q
                        store_q(b + 1, u, k, dst, i)
                    if prep:
                        split_w13(j + AHEAD)
                    if prep > 1:
                        scale_w13(j + (AHEAD + 1), s)

                def w2_high(c, slot):
                    act.wait_ge(w2_scaled, c + 1)
                    nc.scalar.copy(w2r[:].rearrange("p c s n -> p (c s n)")[:, bass.ds(c * 2 * D, D)],
                                   ring[:, slot, :]).then_inc(w2_hi_done, 1)

                both, one = (2, 1) if weights else (0, 0)
                f = following

                def q_of(n):
                    return (n, qt_ctx, n) if f else None

                def q_of_x(n):
                    return (n + TI, qt_x, n) if f else None

                gate_steps(act, 0, Q_FROM, lambda j, k, n: chunk(j, k, both, None))
                gate_steps(act, Q_FROM, Q_FROM + TI, lambda j, k, n: chunk(j, k, both, q_of(n)))
                gate_steps(act, Q_FROM + TI, G_FROM - 1, lambda j, k, n: chunk(j, k, both, q_of_x(n)))
                chunk(G_FROM - 1, (G_FROM - 1) % 2, both, q_of_x(TI - 2))

                chunk(G_FROM, G_FROM % 2, one, q_of_x(TI - 1))
                if weights:
                    done = 0
                    for j, count in enumerate(W2_SPLIT, G_FROM + 1):
                        chunk(j, j % 2, False, None, z0=j == HC - 1)
                        for c in range(done, done + count):
                            if c == done + 2 and j == HC - 1:
                                store_z(b + 1, 0)
                            w2_high(c, c % SLOTS)
                        done += count
                else:
                    gate_steps(act, G_FROM + 1, HC - 1, lambda j, k, n: chunk(j, k, False, None))
                    chunk(HC - 1, (HC - 1) % 2, False, None, z0=following)
                    if following:
                        store_z(b + 1, 0)

            def down_phase(b):
                with act.Fori(1, TI) as i:
                    z_high(b + 1, i, 0)
                    store_z(b + 1, i)

            for t in range(HC):
                dc, hq = t // 4, t % 4
                act.wait_ge(w_in[hq], dc * 16 + 16)
                if t:
                    act.wait_ge(sq_done, t)
                nc.scalar.activation(junk, ring[:, hq, :], ACT.Square,
                                     accum_out=sq2[:, t:t + 1]).then_inc(sq_done, 1)
                if t == HC - 1:
                    norm_w13(0, 0)
                act.wait_ge(w2_turned, t + 1)
                if t >= 2:
                    act.wait_ge(w2_mixed, t - 1)
                nc.scalar.copy(stage[:, t % 2, :], ps_d[:, 0, :]).then_inc(w2_staged, 1)
                if t:
                    s = t - 1
                    act.wait_ge(w2_mixed, s + 1)
                    nc.scalar.copy(w2_f32c[:, 4 * (s % 4):4 * (s % 4) + 4, (s // 4) * P:(s // 4 + 1) * P],
                                   blocks(ps_d[:, 1, :])).then_inc(w2_stored, 1)
                if t in UNIT_AT:
                    u = UNIT_AT.index(t)
                    store_q(0, u, u % 2, qt_ctx if u < TI else qt_x, u % TI)
            z_high(0, 0, 0)
            act.wait_ge(w2_mixed, HC)
            nc.scalar.copy(w2_f32c[:, HC - 4:HC, (KC - 1) * P:KC * P], blocks(ps_d[:, 1, :])).then_inc(w2_stored, 1)
            for i in range(TI):
                if 0 < i < TI - 1:
                    z_high(0, i, i % 2)
                scale_w13(i, i % 2)
                if i == TI - 1:
                    store_z(0, i)
                norm_w13(i + 1, (i + 1) % 2)
                if i < TI - 1:
                    store_z(0, i)
                if i == TI - 2:
                    z_high(0, TI - 1, (TI - 1) % 2)
                split_w13(i)
            scale_w13(AHEAD, AHEAD % 2)
            gate_phase(0, True, True)
            down_phase(0)
            with act.Fori(1, NB - 1) as b:
                gate_phase(b, False, True)
                down_phase(b)
            gate_phase(NB - 1, False, False)

        @block.gpsimd
        def _(pool):
            step = Count()

            def block_max(event, start, n):
                pool.wait_ge(camax_done, event + 1)
                alone(pool)
                nc.gpsimd.partition_all_reduce(cols(cmax, start, n), cols(camax, start, n), P, RMAX).then_inc(cmax_done, 1)

            def round_tile(b, u, k):
                pool.wait_ge(v_done, b * NQ + u + 1)
                nc.gpsimd.tensor_tensor(zb[:, k, :], zb[:, k, :], mb[:, k, :], ALU.add).then_inc(pool_step, 1)
                if not (isinstance(b, int) and b == 0 and u < 2):
                    pool.wait_ge(q_turned, b * NQ + u - 1)
                pool.wait_ge(pool_step, step.next())
                nc.gpsimd.tensor_tensor(qb[:, k, :], zb[:, k, :], mb[:, k, :], ALU.subtract).then_inc(q_done, 1)

            def butterfly(dc, n):
                stride, op = 1 << (n // 2), (ALU.add, ALU.subtract)[n % 2]
                a = w2_f32c[:, :, dc * P:(dc + 1) * P]
                src, dst = (a, fly[:]) if n // 2 % 2 == 0 else (fly[:], a)
                sv = src.rearrange("p (a t r) d -> p a t r d", t=2, r=stride)
                dv = dst.rearrange("p (a t r) d -> p a t r d", t=2, r=stride)
                if n == 0:
                    pool.wait_ge(w2_stored, 4 * dc + 4)
                    if dc:
                        pool.wait_ge(fly_done, dc)
                elif n % 2 == 0:
                    pool.wait_ge(pool_step, step.base + step.n)
                if stride == 1:
                    o, x0, x1 = dv[:, :, n % 2, 0, :], sv[:, :, 0, 0, :], sv[:, :, 1, 0, :]
                elif stride == 8:
                    o, x0, x1 = dv[:, 0, n % 2, :, :], sv[:, 0, 0, :, :], sv[:, 0, 1, :, :]
                else:
                    o, x0, x1 = dv[:, :, n % 2, :, :], sv[:, :, 0, :, :], sv[:, :, 1, :, :]
                last = nc.gpsimd.tensor_tensor(o, x0, x1, op)
                if n < 7:
                    last.then_inc(pool_step, 1)
                    step.next()
                else:
                    last.then_inc(fly_done, 1)

            def w2_scale(c):
                if c == 0:
                    pool.wait_ge(fly_done, KC)
                if c >= SLOTS:
                    pool.wait_ge(w2_lo_done, c - SLOTS + 1)
                nc.gpsimd.tensor_tensor(ring[:, c % SLOTS, :], cols(w2_f32, c * D, D),
                                        cols(rowmul, c, 1).broadcast_to([P, D]), ALU.mult).then_inc(w2_scaled, 1)

            def inverse_root(event, root):
                pool.wait_ge(var_done, event + 1)
                n = root.shape[1]
                nc.gpsimd.tensor_tensor(root, ve[:, 0:n], half[:, 0:n], ALU.pow).then_inc(root_done, 1)

            nc.gpsimd.memset(half[:], -0.5).then_inc(pool_step, 1)
            pool.wait_ge(pool_step, step.next())
            block_max(0, 0, KC)
            for i in range(1, TI):
                block_max(i, i * KC, KC)
                round_tile(0, i - 1, (i - 1) % 2)
            inverse_root(root_event(0, None), rs1[:])
            for u in range(TI - 1, NQ):
                round_tile(0, u, u % 2)
            flown = iter(range(8 * KC))

            def butterflies(count):
                for _ in range(count):
                    m = next(flown)
                    butterfly(m // 8, m % 8)

            for i, count in enumerate(FLY_ROOTS):
                butterflies(count)
                inverse_root(root_event(0, i), rs2[:, i:i + 1])
            butterflies(FLY_MAX)
            block_max(TI, 0, TI * KC)
            butterflies(FLY_X)
            inverse_root(root_event(1, None), rs1[:])
            for u in range(NQ):
                round_tile(1, u, u % 2)
                butterflies(FLY_UNITS[u])
            assert next(flown, None) is None
            pool.wait_ge(peaks_done, 1)
            nc.gpsimd.partition_all_reduce(gpeaks[:], peaks[:], P, RMAX).then_inc(gpeaks_done, 1)
            pool.wait_ge(rowmul_done, 1)
            pool.wait_ge(w13_turned, 2 * HC)
            for c in range(HC):
                w2_scale(c)
                if c == HC - W2_SPLIT[-1]:
                    inverse_root(root_event(1, 0), rs2[:, 0:1])
            for i in range(1, TI):
                inverse_root(root_event(1, i), rs2[:, 0:1])
            with pool.Fori(2, NB) as b:
                block_max(b + (TI - 1), 0, TI * KC)
                inverse_root(root_event(b, None), rs1[:])
                with step.loop(b - 2, NB - 2, NQ), pool.Fori(0, NQ // 2) as r, step.loop(r, NQ // 2, 2):
                    for k in range(2):
                        round_tile(b, r * 2 + k, k)
                for i in range(TI):
                    inverse_root(root_event(b, i), rs2[:, 0:1])

        @block.vector
        def _(dve):
            step = Count()

            def variance(var):
                dve.wait_ge(dve_step, step.base + step.n)
                nc.vector.tensor_scalar(ve[:, 0:var.shape[1]], var, LN_EPS, None, ALU.add).then_inc(var_done, 1)

            def stats_start(src, i):
                alone(dve)
                nc.vector.bn_stats(bn[:, i, :], src).then_inc(dve_step, 1)
                return step.next()

            def stats_end(started, i, mv):
                dve.wait_ge(dve_step, started)
                alone(dve)
                nc.vector.bn_aggr(mv, bn[:, i, :]).then_inc(dve_step, 1)
                return step.next()

            def x_stats(b, tiles):
                started = []
                for i in tiles:
                    dve.wait_ge(x_in[i], b * 16 + 16)
                    started.append(stats_start(x_tile(b, i), i))
                for i, at in zip(tiles, started):
                    stats_end(at, i, mv1[:, i, :])

            def context_max(tiles):
                a, n = tiles.start, len(tiles)
                nc.vector.tensor_reduce(cols(camax, a * KC, n * KC),
                                        cols(ctx_sb, a * D, n * D).rearrange("p (k n) -> p k n", n=P), AX_X, ALU.max,
                                        apply_absolute_value=True).then_inc(camax_done, 1)

            def inverse_scales(peak, eps, safe, inverse, scales):
                nc.vector.tensor_scalar(safe, peak, eps, None, ALU.max).then_inc(dve_step, 1)
                dve.wait_ge(dve_step, step.next())
                nc.vector.reciprocal(inverse, safe).then_inc(dve_step, 1)
                nc.vector.tensor_scalar(scales, safe, 1.0 / FP8_MAX, None, ALU.mult).then_inc(dve_step, 1)
                step.next()
                dve.wait_ge(dve_step, step.next())
                nc.vector.tensor_scalar(inverse, inverse, FP8_MAX, None, ALU.mult).then_inc(dve_step, 1)
                dve.wait_ge(dve_step, step.next())

            def context_scales(event, start, n):
                dve.wait_ge(cmax_done, event + 1)
                c = cols(cmax, start, n)
                inverse_scales(c, W_EPS, cols(camax, start, n), c, cols(sw, start, n))

            def scale_and_rounders(src, inverse, k, done, reached):
                z = zb[:, k, :]
                nc.vector.tensor_tensor(blocks(z), blocks(src), inverse.unsqueeze(2).broadcast_to([P, KC, P]),
                                        ALU.mult).then_inc(done, 1)
                dve.wait_ge(done, reached())
                nc.vector.tensor_scalar(mb[:, k, :].bitcast(I32), z.bitcast(I32), EXPONENT, None,
                                        ALU.bitwise_and).then_inc(dve_step, 1)
                dve.wait_ge(dve_step, step.next())
                nc.vector.tensor_scalar(mb[:, k, :], mb[:, k, :], LEAST_NORMAL, ROUNDER, ALU.max,
                                        ALU.mult).then_inc(v_done, 1)

            def buffers_free(b, u):
                dve.wait_ge(q_done, b * NQ + u - 1)

            def quantise_context(b, i, k):
                scale_and_rounders(cols(ctx_sb, i * D, D), cols(cmax, i * KC, KC), k, ctx_read, lambda: b * TI + i + 1)

            def normalise_tokens(b, i, k):
                nc.vector.tensor_scalar(zb[:, k, :], x_tile(b, i), mv1[:, i, 0:1], rs1[:, i:i + 1], ALU.subtract,
                                        ALU.mult).then_inc(dve_step, 1)
                dve.wait_ge(dve_step, step.next())
                nc.vector.tensor_reduce(xamax[:], blocks(zb[:, k, :]), AX_X, ALU.max,
                                        apply_absolute_value=True).then_inc(dve_step, 1)
                step.next()

            def quantise_tokens(i, k):
                dve.wait_ge(dve_step, step.base + step.n)
                inverse_scales(xamax[:], ACT_EPS, safe[:], rq[:], cols(sx, i * KC, KC))
                scale_and_rounders(zb[:, k, :], rq[:], k, dve_step, step.next)

            def block_scales():
                shape = [P, TI, KC, TI]
                a = sx[:].rearrange("p (i k) -> p i k", i=TI).unsqueeze(3).broadcast_to(shape)
                w = sw[:].rearrange("p (n k) -> p k n", n=TI).unsqueeze(1).broadcast_to(shape)
                nc.vector.tensor_tensor(coef[:].rearrange("p (i k n) -> p i k n", i=TI, k=KC), a, w,
                                        ALU.mult).then_inc(dve_step, 1)
                dve.wait_ge(dve_step, step.next())
                alone(dve)

            def add_product(b, i, kb, bank):
                g = (b * TI + i) * KC + kb
                dve.wait_ge(g_ready, g + 1)
                for half_done in (g_half_used, g_used):
                    if not isinstance(g, int) or g > 0:
                        dve.wait_ge(half_done, g)
                    for nb in (0, 1) if half_done is g_half_used else (2, 3):
                        y = cols(x_sb, (par(b) * TI + i) * D + nb * P, P)
                        last = nc.vector.scalar_tensor_tensor(
                            out=y, in0=bank[:, nb * P:(nb + 1) * P], scalar=cols(coef, (i * KC + kb) * TI + nb, 1),
                            in1=y, op0=ALU.mult, op1=ALU.add)
                    last.then_inc(half_done, 1)

            def y_stats_start(b, i):
                dve.wait_ge(g_used, (b * TI + i) * KC + KC)
                return stats_start(x_tile(b, i), 0)

            def y_stats(b, i, mv):
                stats_end(y_stats_start(b, i), 0, mv)

            def normalise(b, i, k, mv, root, free):
                if free is not None:
                    dve.wait_ge(zlo_done, free)
                nc.vector.tensor_scalar(zb[:, k, :], x_tile(b, i), mv, root, ALU.subtract,
                                        ALU.mult).then_inc(zn_done, 1)

            def z_low(b, i, k):
                dve.wait_ge(zhi_done, b * TI + i + 1)
                dve.wait_ge(zn_done, b * TI + i + 1)
                nc.vector.scalar_tensor_tensor(out=z_hl[:, 1, :], in0=zb[:, k, :], scalar=Z_SCALE, in1=z_hl[:, 0, :],
                                               op0=ALU.mult, op1=ALU.subtract).then_inc(zlo_done, 1)

            def bits(dst, src, n, m, done):
                nc.vector.tensor_scalar(dst.bitcast(I32), src.bitcast(I32), float(n), float(m), ALU.mult,
                                        ALU.add).then_inc(done, 1)

            def scales_w13(j):
                dve.wait_ge(sq_done, j * 2 + (2 + HC))
                t = cols(tb13, j * 2, 2)
                nc.vector.tensor_scalar(t.bitcast(I32), cols(sq13, j * 2, 2).bitcast(I32), 24, 23,
                                        ALU.logical_shift_right, ALU.logical_shift_left).then_inc(dve_step, 1)
                dve.wait_ge(dve_step, step.next())
                bits(cols(silu_sc, j, 1), cols(tb13, j * 2, 1), 1, 39 * ONE, dve_step)
                bits(cols(hid_sc, j, 1), cols(tb13, j * 2, 1), -1, 169 * ONE, dve_step)
                step.next()
                step.next()
                bits(cols(sc13, j * 2, 2), t, -1, 204 * ONE, sc13_done)

            def low_w13(j):
                for w in range(2):
                    dve.wait_ge(w13_hi_done, j * 2 + w + 1)
                    at = (slice(None), w, slice(None), bass.ds(j * P, P))
                    nc.vector.tensor_tensor(w13_lo[at], blocks(ps_d[:, w, :]), w13_hi[at],
                                            ALU.subtract).then_inc(w13_lo_done, 1)

            def hidden(b, j, k):
                dve.wait_ge(silu_done, b * HC + (j + 1) + 2)
                dve.wait_ge(up_ready, b * HC + j + 1)
                nc.vector.scalar_tensor_tensor(out=hid[:, k, :], in0=hid[:, k, :], scalar=cols(hid_sc, j, 1),
                                               in1=ps_u[:, k, :], op0=ALU.mult, op1=ALU.mult).then_inc(hid_done, 1)

            def hidden_low(b, j, k):
                dve.wait_ge(hhi_done, b * HC + j + 1)
                nc.vector.tensor_tensor(cols(h_lo, j * S, S), hid[:, k, :], cols(h_hi, j * S, S),
                                        ALU.subtract).then_inc(hlo_done, 1)

            def w2_low(c, slot):
                dve.wait_ge(w2_hi_done, c + 1)
                flat = w2r[:].rearrange("p c s n -> p (c s n)")
                nc.vector.tensor_tensor(flat[:, bass.ds(c * 2 * D + D, D)], ring[:, slot, :],
                                        flat[:, bass.ds(c * 2 * D, D)], ALU.subtract).then_inc(w2_lo_done, 1)

            def weight_scales():
                dve.wait_ge(w_scaled, 2 * HC)
                bits(sc13[:], tb13[:], 1, 50 * ONE, dve_step)
                dve.wait_ge(dve_step, step.next())
                pair = sc13[:].rearrange("p (j w) -> p w j", w=2)
                nc.vector.tensor_tensor(rowmul[:], pair[:, 0, :], pair[:, 1, :], ALU.mult).then_inc(dve_step, 1)
                dve.wait_ge(dve_step, step.next())
                dve.wait_ge(sq_done, HC)
                nc.vector.tensor_reduce(peaks[:, 0:1], sq2[:], AX_X, ALU.max).then_inc(dve_step, 1)
                dve.wait_ge(dve_step, step.next())
                nc.vector.tensor_reduce(peaks[:, 1:2], rowmul[:], AX_X, ALU.max).then_inc(peaks_done, 1)
                dve.wait_ge(gpeaks_done, 1)
                nc.vector.tensor_scalar(gs[:, 0:1].bitcast(I32), gpeaks[:, 0:1].bitcast(I32), 24, 23,
                                        ALU.logical_shift_right, ALU.logical_shift_left).then_inc(dve_step, 1)
                dve.wait_ge(dve_step, step.next())
                bits(gs[:, 1:2], gs[:, 0:1], -1, 198 * ONE, dve_step)
                bits(gs[:, 2:3], gs[:, 0:1], 1, 50 * ONE, dve_step)
                bits(gs[:, 3:4], gpeaks[:, 1:2], -1, 254 * ONE, dve_step)
                step.next()
                step.next()
                dve.wait_ge(dve_step, step.next())
                nc.vector.tensor_scalar(rowmul[:], rowmul[:], gs[:, 3:4], gs[:, 1:2], ALU.mult,
                                        ALU.mult).then_inc(rowmul_done, 1)
                nc.vector.tensor_scalar(outmul[:], gpeaks[:, 1:2], 2.0 ** 30 / float(H) ** 0.5, gs[:, 2:3], ALU.mult,
                                        ALU.mult).then_inc(dve_step, 1)
                dve.wait_ge(dve_step, step.next())

            def gate_phase(b, weights, following):
                def chunk(j, k, prep, ahead, between, after):
                    ahead()
                    if prep:
                        low_w13(j + (AHEAD - 1))
                    hidden(b, j, k)
                    if prep > 1:
                        scales_w13(j + (AHEAD + 1))
                    between()
                    hidden_low(b, j, k)
                    after()

                def nothing():
                    pass

                both, one = (2, 1) if weights else (0, 0)
                p = 3 * weights
                q0 = Q_FROM - 1
                if not following:
                    gate_steps(dve, 0, HC, lambda j, k, n: chunk(j, k, 0, nothing, nothing, nothing))
                    return

                for i in range(TI):
                    dve.wait_ge(ctx_in[i], b * 16 + 32)
                context_max(range(TI))
                early = TI // 2 if weights else 0
                x_stats(b + 1, range(early))
                chunk(0, 0, both, nothing, nothing, nothing)
                context_scales(b + TI, 0, TI * KC)
                for j in (1, 2):
                    now = (early + j - 1,) if weights else (2 * j - 2, 2 * j - 1)
                    chunk(j, j % 2, both, nothing, lambda: x_stats(b + 1, now[:1]), lambda: x_stats(b + 1, now[1:]))
                variance(mv1[:, :, 1])

                def context_unit(j, k, n):
                    def unit():
                        buffers_free(b + 1, n)
                        quantise_context(b + 1, n, (k + 1) % 2)
                    chunk(j, k, both, unit, nothing, nothing)

                gate_steps(dve, q0, q0 + TI, context_unit, step, p + 1)
                dve.wait_ge(root_done, root_event(b + 1, None) + 1)
                alone(dve)

                def token_start(i):
                    buffers_free(b + 1, TI + i)
                    normalise_tokens(b + 1, i, i % 2)

                token_start(0)
                for i in range(TI):
                    chunk(q0 + TI + i, (q0 + i) % 2, both, lambda: quantise_tokens(i, i % 2),
                          (lambda: token_start(i + 1)) if i < TI - 1 else nothing, nothing)
                block_scales()

                def product_chunk(j, k, n, prep=0):
                    chunk(j, k, prep, lambda: add_product(b + 1, 0, n, ps_x[:, (k + 1) % 2, :]), nothing, nothing)

                def split_w2(c0, c1):
                    for c in range(c0, c1):
                        w2_low(c, c % SLOTS)

                done = 0
                if weights:
                    product_chunk(G_FROM, G_FROM % 2, 0, one)
                    weight_scales()
                    for n in range(1, KC):
                        product_chunk(G_FROM + n, (G_FROM + n) % 2, n, one if n == 1 else 0)
                        split_w2(done, done + W2_SPLIT[n - 1])
                        done += W2_SPLIT[n - 1]
                else:
                    gate_steps(dve, G_FROM, G_FROM + KC, product_chunk)
                y_stats(b + 1, 0, mv2[:, 0, :])
                variance(mv2[:, 0, 1:2])
                dve.wait_ge(root_done, root_event(b + 1, 0) + 1)
                normalise(b + 1, 0, 0, mv2[:, 0, 0:1], rs2[:, 0:1], (b + 1) * TI)
                chunk(HC - 1, (HC - 1) % 2, 0, nothing, lambda: z_low(b + 1, 0, 0), nothing)
                if weights:
                    split_w2(done, HC)

            def down_phase(b, following):
                def z_of(i):
                    dve.wait_ge(root_done, root_event(b + 1, i) + 1)
                    normalise(b + 1, i, 0, mv2[:, 0, 0:1], rs2[:, 0:1], (b + 1) * TI + i)
                    z_low(b + 1, i, 0)

                def store(i):
                    dve.wait_ge(down_ready, b * TI + i + 1)
                    y = x_tile(b, i)
                    nc.vector.scalar_tensor_tensor(out=y, in0=d_bank(i), scalar=outmul[:, 0:1], in1=y,
                                                   op0=ALU.mult, op1=ALU.add).then_inc(out_ready, 1)

                with dve.Fori(0, TI - 1) as i, step.loop(i, TI - 1, 2 * following):
                    if following:
                        for kb in range(KC):
                            add_product(b + 1, i + 1, kb, ps_x[:, kb % 2, :])
                        y_stats(b + 1, i + 1, mv2[:, 0, :])
                        variance(mv2[:, 0, 1:2])
                        z_of(i + 1)
                    store(i)
                store(TI - 1)

            for n, freed in enumerate((silu_done, hid_done, hlo_done, out_ready)):
                nc.vector.memset(credit[:, n:n + 1], 0.0).then_inc(freed, 2)

            dve.wait_ge(ctx_in[0], 16)
            context_max(range(1))
            for i in range(TI):
                if i + 1 < TI:
                    dve.wait_ge(ctx_in[i + 1], 16)
                    context_max(range(i + 1, i + 2))
                if i >= 2:
                    buffers_free(0, i)
                context_scales(i, i * KC, KC)
                quantise_context(0, i, i % 2)
                if i == TI - 2:
                    x_stats(0, range(TI))
                    variance(mv1[:, :, 1])
            dve.wait_ge(root_done, root_event(0, None) + 1)
            for i in range(TI):
                buffers_free(0, TI + i)
                normalise_tokens(0, i, i % 2)
                quantise_tokens(i, i % 2)
            block_scales()

            def first_z(i):
                dve.wait_ge(root_done, root_event(0, i) + 1)
                normalise(0, i, i % 2, mv2[:, i, 0:1], rs2[:, i:i + 1], i - 1 if i > 1 else None)

            for i in range(TI):
                for kb in range(KC):
                    add_product(0, i, kb, (ps_g if kb < 2 else ps_u)[:, kb % 2, :])
                    if i and kb == 1:
                        first_z(i - 1)
                started = y_stats_start(0, i)
                if i:
                    scales_w13(i - 1)
                stats_end(started, 0, mv2[:, i, :])
                if i:
                    z_low(0, i - 1, (i - 1) % 2)
                variance(mv2[:, i, 1:2])
                if i > 1:
                    low_w13(i - 2)
            first_z(TI - 1)
            scales_w13(AHEAD - 1)
            z_low(0, TI - 1, (TI - 1) % 2)
            low_w13(AHEAD - 2)
            scales_w13(AHEAD)
            gate_phase(0, True, True)
            down_phase(0, True)
            with dve.Fori(1, NB - 1) as b:
                with step.loop(b - 1, NB - 2, 4 + TI * 2 + TI * 1 + TI * 8 + 1 + TI * 2):
                    gate_phase(b, False, True)
                    down_phase(b, True)
            gate_phase(NB - 1, False, False)
            down_phase(NB - 1, False)


_INS = ["x", "ctx_2048", "L0_ffn_W1", "L0_ffn_W2", "L0_ffn_W3"]


def kernel(**inputs):
    import numpy as _np
    import concourse.bacc as _bacc
    from concourse import mybir as _mybir
    from concourse.bass_utils import run_bass_kernel_spmd as _run

    nc = _bacc.Bacc("TRN2", target_bir_lowering=False, num_devices=1)
    i = _np.arange(128)
    odd = _np.array([[bin(a & b).count("1") % 2 for b in i] for a in i])
    consts = {
        "eye32": _np.eye(128, dtype=_np.float32),
        "eye16": _np.eye(128, dtype=_np.float16),
        "had": (1 - 2 * odd).astype(_np.float32),
    }
    arrays, aps = {}, {}
    for name, a in [(n, _np.ascontiguousarray(inputs[n])) for n in _INS] + list(consts.items()):
        arrays[f"in_{name}_dram"] = a
        aps[name] = nc.dram_tensor(f"in_{name}_dram", a.shape, _mybir.dt.from_np(a.dtype), kind="ExternalInput").ap()
    shape = inputs["x"].shape
    out = nc.dram_tensor("out_0_dram", shape, _mybir.dt.float32, kind="ExternalOutput").ap()
    xattn_ffn(nc, aps["x"], aps["ctx_2048"], aps["L0_ffn_W1"], aps["L0_ffn_W2"], aps["L0_ffn_W3"],
              aps["eye32"], aps["eye16"], aps["had"], out)
    r = _run(nc, [arrays], core_ids=[0])
    return r.results[0]["out_0_dram"]
```
